# Optimizing a Trainium2 kernel written in Bass

```python
import numpy as np
import jax
import jax.numpy as jnp

def _softmax(x, axis=-1):
    return jax.nn.softmax(x, axis=axis)

def _gelu(x):
    return jax.nn.gelu(x, approximate=True)

def _silu(x):
    return jax.nn.silu(x)

def _sigmoid(x):
    return jax.nn.sigmoid(x)

def _layernorm(x, axis=-1, eps=1e-05):
    m = jnp.mean(x, axis=axis, keepdims=True)
    v = jnp.var(x, axis=axis, keepdims=True)
    return (x - m) / jnp.sqrt(v + eps)

def _scatter_add(tgt, idx, src, axis=0):
    return tgt.at[idx].add(src)

def _segment_sum(src, seg, n):
    return jax.ops.segment_sum(src, seg, n)
kernel_name = 'mk_seq_postln_d1_jaxref_r8_363954'

def setup_inputs(seed: int=0):
    np.random.seed(seed)
    _w = jnp.asarray

    def _L0_attn_setup():
        import jax, jax.numpy as jnp
        import numpy as np
        EPS = 1e-05

        def _layernorm(x, gamma, beta):
            m = jnp.mean(x, axis=-1, keepdims=True)
            v = jnp.mean(jnp.square(x - m), axis=-1, keepdims=True)
            return (x - m) * jax.lax.rsqrt(v + EPS) * gamma + beta
        key = jax.random.key(seed)
        B, Q, C, H = (4, 512, 128, 16)
        hd = C // H
        ks = jax.random.split(key, 8)
        s_in = 1.0 / np.sqrt(C)
        return {'x': jax.random.normal(ks[0], (B, Q, C), jnp.float32), 'qkv_w': jax.random.normal(ks[1], (3 * C, C), jnp.float32) * s_in, 'qkv_b': jnp.zeros((3 * C,), jnp.float32), 'kn_g': jnp.ones((hd,), jnp.float32), 'kn_b': jnp.zeros((hd,), jnp.float32), 'vn_g': jnp.ones((hd,), jnp.float32), 'vn_b': jnp.zeros((hd,), jnp.float32), 'temperature': jnp.ones((H, 1, 1), jnp.float32), 'attn_bias': jnp.zeros((H, hd, hd), jnp.float32), 'p1_w': jax.random.normal(ks[2], (C, C), jnp.float32) * s_in, 'p1_b': jnp.zeros((C,), jnp.float32), 'p2_w': jax.random.normal(ks[3], (C, C), jnp.float32) * s_in, 'p2_b': jnp.zeros((C,), jnp.float32)}
    _L0_attn_in = _L0_attn_setup()

    def _L0_ffn_setup():
        import jax, jax.numpy as jnp
        import numpy as np
        from jax import lax
        HIDDEN = 128
        INTER = 64
        E = 64
        K = 6
        G = 8
        TG = 4
        NSH = 2
        ISH = INTER * NSH

        def _moe_forward(hidden_states, gate_w, gate_bias, eg_w, eu_w, ed_w, sg_w, su_w, sd_w):
            B, S, H = hidden_states.shape
            x = hidden_states.reshape(-1, H)
            T = x.shape[0]
            shared = jax.nn.silu(x @ sg_w.T) * (x @ su_w.T) @ sd_w.T
            logits = x @ gate_w.T
            scores = jax.nn.sigmoid(logits) + gate_bias
            group_scores = scores.reshape(T, G, E // G).max(axis=-1)
            _, sel_groups = lax.top_k(group_scores, TG)
            group_mask = jnp.zeros((T, G), scores.dtype).at[jnp.arange(T)[:, None], sel_groups].set(1.0)
            mask = jnp.repeat(group_mask, E // G, axis=1)
            masked_scores = scores * mask
            topk_w, topk_i = lax.top_k(masked_scores, K)
            topk_w = topk_w / (topk_w.sum(axis=-1, keepdims=True) + 1e-08)
            comb = jnp.zeros((T, E), x.dtype).at[jnp.arange(T)[:, None], topk_i].add(topk_w)
            h = jax.nn.silu(jnp.einsum('th,eih->eti', x, eg_w)) * jnp.einsum('th,eih->eti', x, eu_w)
            routed = jnp.einsum('eti,ehi,te->th', h, ed_w, comb)
            return (shared + routed).reshape(B, S, H)
        key = jax.random.key(seed)
        ks = jax.random.split(key, 9)
        s = 0.02
        return {'hidden_states': jax.random.normal(ks[0], (1, 128, HIDDEN), jnp.float32), 'gate_w': jax.random.normal(ks[1], (E, HIDDEN), jnp.float32) * s, 'gate_bias': jnp.zeros((E,), jnp.float32), 'eg_w': jax.random.normal(ks[2], (E, INTER, HIDDEN), jnp.float32) * s, 'eu_w': jax.random.normal(ks[3], (E, INTER, HIDDEN), jnp.float32) * s, 'ed_w': jax.random.normal(ks[4], (E, HIDDEN, INTER), jnp.float32) * s, 'sg_w': jax.random.normal(ks[5], (ISH, HIDDEN), jnp.float32) * s, 'su_w': jax.random.normal(ks[6], (ISH, HIDDEN), jnp.float32) * s, 'sd_w': jax.random.normal(ks[7], (HIDDEN, ISH), jnp.float32) * s}
    _L0_ffn_in = _L0_ffn_setup()
    _d = {'L0_attn_x': _L0_attn_in['x'], 'L0_attn_qkv_w': _L0_attn_in['qkv_w'], 'L0_attn_qkv_b': _L0_attn_in['qkv_b'], 'L0_attn_kn_g': _L0_attn_in['kn_g'], 'L0_attn_kn_b': _L0_attn_in['kn_b'], 'L0_attn_vn_g': _L0_attn_in['vn_g'], 'L0_attn_vn_b': _L0_attn_in['vn_b'], 'L0_attn_temperature': _L0_attn_in['temperature'], 'L0_attn_attn_bias': _L0_attn_in['attn_bias'], 'L0_attn_p1_w': _L0_attn_in['p1_w'], 'L0_attn_p1_b': _L0_attn_in['p1_b'], 'L0_attn_p2_w': _L0_attn_in['p2_w'], 'L0_attn_p2_b': _L0_attn_in['p2_b'], 'L0_ffn_gate_w': _L0_ffn_in['gate_w'], 'L0_ffn_gate_bias': _L0_ffn_in['gate_bias'], 'L0_ffn_eg_w': _L0_ffn_in['eg_w'], 'L0_ffn_eu_w': _L0_ffn_in['eu_w'], 'L0_ffn_ed_w': _L0_ffn_in['ed_w'], 'L0_ffn_sg_w': _L0_ffn_in['sg_w'], 'L0_ffn_su_w': _L0_ffn_in['su_w'], 'L0_ffn_sd_w': _L0_ffn_in['sd_w']}
    _x0 = _d['L0_attn_x']
    _d['L0_attn_x'] = jax.random.normal(jax.random.fold_in(jax.random.key(seed), 1), (8, 512, 128), dtype=_x0.dtype)
    del _x0
    return _d

def reference(L0_attn_x, L0_attn_qkv_w, L0_attn_qkv_b, L0_attn_kn_g, L0_attn_kn_b, L0_attn_vn_g, L0_attn_vn_b, L0_attn_temperature, L0_attn_attn_bias, L0_attn_p1_w, L0_attn_p1_b, L0_attn_p2_w, L0_attn_p2_b, L0_ffn_gate_w, L0_ffn_gate_bias, L0_ffn_eg_w, L0_ffn_eu_w, L0_ffn_ed_w, L0_ffn_sg_w, L0_ffn_su_w, L0_ffn_sd_w):

    def _L0_attn_ref(x, qkv_w, qkv_b, kn_g, kn_b, vn_g, vn_b, temperature, attn_bias, p1_w, p1_b, p2_w, p2_b):
        import jax, jax.numpy as jnp
        import numpy as np
        EPS = 1e-05

        def _layernorm(x, gamma, beta):
            m = jnp.mean(x, axis=-1, keepdims=True)
            v = jnp.mean(jnp.square(x - m), axis=-1, keepdims=True)
            return (x - m) * jax.lax.rsqrt(v + EPS) * gamma + beta
        B, Q, C = x.shape
        H = temperature.shape[0]
        hd = C // H
        qkv = (x @ qkv_w.T + qkv_b).reshape(B, Q, 3, H, hd)
        qkv = jnp.transpose(qkv, (2, 0, 3, 1, 4))
        q, k, v = (qkv[0], qkv[1], qkv[2])
        k = _layernorm(k, kn_g, kn_b)
        v = _layernorm(v, vn_g, vn_b)
        kv = jnp.einsum('bhqd,bhqe->bhde', k, v) / Q * temperature + attn_bias
        att = jnp.einsum('bhqd,bhde->bhqe', q, kv)
        att = jnp.transpose(att, (0, 2, 1, 3)).reshape(B, Q, C) + x
        h = jax.nn.gelu(att @ p1_w.T + p1_b, approximate=False)
        return h @ p2_w.T + p2_b + x

    def _L0_ffn_ref(hidden_states, gate_w, gate_bias, eg_w, eu_w, ed_w, sg_w, su_w, sd_w):
        import jax, jax.numpy as jnp
        import numpy as np
        from jax import lax
        HIDDEN = 128
        INTER = 64
        E = 64
        K = 6
        G = 8
        TG = 4
        NSH = 2
        ISH = INTER * NSH

        def _moe_forward(hidden_states, gate_w, gate_bias, eg_w, eu_w, ed_w, sg_w, su_w, sd_w):
            B, S, H = hidden_states.shape
            x = hidden_states.reshape(-1, H)
            T = x.shape[0]
            shared = jax.nn.silu(x @ sg_w.T) * (x @ su_w.T) @ sd_w.T
            logits = x @ gate_w.T
            scores = jax.nn.sigmoid(logits) + gate_bias
            group_scores = scores.reshape(T, G, E // G).max(axis=-1)
            _, sel_groups = lax.top_k(group_scores, TG)
            group_mask = jnp.zeros((T, G), scores.dtype).at[jnp.arange(T)[:, None], sel_groups].set(1.0)
            mask = jnp.repeat(group_mask, E // G, axis=1)
            masked_scores = scores * mask
            topk_w, topk_i = lax.top_k(masked_scores, K)
            topk_w = topk_w / (topk_w.sum(axis=-1, keepdims=True) + 1e-08)
            comb = jnp.zeros((T, E), x.dtype).at[jnp.arange(T)[:, None], topk_i].add(topk_w)
            h = jax.nn.silu(jnp.einsum('th,eih->eti', x, eg_w)) * jnp.einsum('th,eih->eti', x, eu_w)
            routed = jnp.einsum('eti,ehi,te->th', h, ed_w, comb)
            return (shared + routed).reshape(B, S, H)
        return _moe_forward(hidden_states, gate_w, gate_bias, eg_w, eu_w, ed_w, sg_w, su_w, sd_w)
    x = L0_attn_x
    x = _layernorm(x + _L0_attn_ref(x, L0_attn_qkv_w, L0_attn_qkv_b, L0_attn_kn_g, L0_attn_kn_b, L0_attn_vn_g, L0_attn_vn_b, L0_attn_temperature, L0_attn_attn_bias, L0_attn_p1_w, L0_attn_p1_b, L0_attn_p2_w, L0_attn_p2_b), axis=-1)
    x = _layernorm(x + _L0_ffn_ref(x, L0_ffn_gate_w, L0_ffn_gate_bias, L0_ffn_eg_w, L0_ffn_eu_w, L0_ffn_ed_w, L0_ffn_sg_w, L0_ffn_su_w, L0_ffn_sd_w), axis=-1)
    return x

_drawn_inputs = setup_inputs


def setup_inputs(seed=0):
    import zlib

    import numpy as np

    out = dict(_drawn_inputs(seed))
    spreads = {'L0_attn_qkv_b': (0.0, 0.355),
     'L0_attn_kn_g': (1.0, 0.6),
     'L0_attn_kn_b': (0.0, 0.563),
     'L0_attn_vn_g': (1.0, 0.6),
     'L0_attn_vn_b': (0.0, 0.787),
     'L0_attn_temperature': (1.0, 0.6),
     'L0_attn_attn_bias': (0.0, 0.1),
     'L0_attn_p1_b': (0.0, 0.274),
     'L0_attn_p2_b': (0.0, 0.1),
     'L0_ffn_gate_bias': (0.0, 0.8)}
    factors = {'L0_ffn_gate_w': 8.0,
     'L0_ffn_eg_w': 8.0,
     'L0_ffn_eu_w': 8.0,
     'L0_ffn_ed_w': 8.0,
     'L0_ffn_sg_w': 8.0,
     'L0_ffn_su_w': 8.0,
     'L0_ffn_sd_w': 8.0}
    for name, (base, spread) in spreads.items():
        noise = np.random.default_rng([zlib.crc32(name.encode()), seed]).standard_normal(out[name].shape)
        drawn = base * np.exp(spread * noise) if base else spread * noise
        out[name] = jnp.asarray(drawn.astype(out[name].dtype))
    for name, factor in factors.items():
        out[name] = (out[name] * factor).astype(out[name].dtype)
    return out
```

```python
from contextlib import ExitStack

import concourse.bass as bass
from concourse import mybir


def post_ln_block(
    nc: bass.Bass,
    x_t: bass.AP,
    proj: bass.AP,
    cols: bass.AP,
    rows: bass.AP,
    moe_w: bass.AP,
    out: bass.AP,
):
    fp32 = mybir.dt.float32
    f32r = mybir.dt.float32r
    i32 = mybir.dt.int32
    ALU = mybir.AluOpType
    ACT = mybir.ActivationFunctionType
    AX = mybir.AxisListType

    NB, C, T = x_t.shape
    P = 128
    HD = 8
    NH = C // HD
    NT = T // P
    E = 64
    NG, TOPG, TOPK = 8, 4, 6
    EG = E // NG
    NS = moe_w.shape[2] // P
    SP3 = 3
    PC = NS // SP3
    EPS = 1e-5
    PAD = -3.0e38
    LAG = 3
    R = 3

    ctx = ExitStack()
    with ctx:
        def sb(name, shape, dt=fp32):
            return ctx.enter_context(nc.sbuf_tensor(name, shape, dt))

        def ps(name):
            return ctx.enter_context(nc.psum_tensor(name, [P, T], fp32))

        def sem(name):
            return ctx.enter_context(nc.semaphore(name))

        moe_hi = [sb(f"moe_hi{m}", [P, NS * P], f32r) for m in range(3)]
        moe_lo = [sb(f"moe_lo{m}", [P, NS * P], f32r) for m in range(3)]
        work = sb("work", [P, 3 * R, T])
        silu = [work[:, i, :] for i in range(R)]
        scaled = [work[:, R + i, :] for i in range(R)]
        hid = [work[:, 2 * R + i, :] for i in range(R)]
        stage = [work[:, 3 * i:3 * i + 3, :].rearrange("p a t -> p (a t)")[:, 0:PC * P]
                 .rearrange("p (j h) -> p j h", h=P) for i in range(3)]
        stage_mean = sb("stage_mean", [P, PC])
        PW = proj.shape[1]
        QO, KO, P1O, P2O, GO = 0, C, 3 * C, 4 * C, 5 * C
        shared = sb("shared", [P, 2 * T])
        proj_f = shared[:, 0:PW]
        kv_sq = shared[:, :].rearrange("p (t c) -> p t c", c=2 * C)
        att, ffn = shared[:, 0:T], shared[:, T:2 * T]
        proj_hi = sb("proj_hi", [P, PW], f32r)
        proj_lo = sb("proj_lo", [P, PW], f32r)
        col = sb("col", [P, cols.shape[1]])
        b_q, b_1, b_2, temp, g_k, b_k = [col[:, i:i + 1] for i in range(6)]
        att_bias = col[:, 6:6 + HD]
        row = sb("row", [P, rows.shape[0]])
        b_kv = row[:, 0:2 * C]
        g_v, b_v = row[:, 2 * C:3 * C], row[:, 3 * C:4 * C]
        b_gate = row[:, 4 * C:4 * C + E]
        mean_kv = sb("mean_kv", [P, 2 * NH])
        mean_b = sb("mean_b", [P, 2 * NH])
        mean_p2 = sb("mean_p2", [P, 1])
        neg_p2 = sb("neg_p2", [P, 1])
        b_2c = sb("b_2c", [P, 1])

        ident = sb("ident", [P, P])
        centre_f = sb("centre_f", [P, P])
        centre = sb("centre", [P, P], f32r)
        centre2 = sb("centre2", [P, P], f32r)
        ones_f = sb("ones_f", [P, P])
        ones_r = sb("ones_r", [P, P], f32r)
        blocks = sb("blocks", [P, NH, HD])
        m_kv, m_k, m_v, m_1 = [sb(f"m_{i}", [P, P]) for i in range(4)]

        xt = sb("xt", [P, T])
        x_hi, x_lo = sb("x_hi", [P, T], f32r), sb("x_lo", [P, T], f32r)
        kv_room = sb("kv_room", [P, NT * 2 * C])
        kv = kv_room[:, :].rearrange("p (t c) -> p t c", c=2 * C)
        cen = kv_room[:, 0:T]
        xn_tok = kv_room[:, T:2 * T].rearrange("p (t c) -> p t c", c=C)
        held = sb("held", [P, 1])
        NK = NT * 2 * NH
        KV, LN2, LN1 = slice(0, NK), slice(NK, NK + NT), slice(NK + NT, NK + 2 * NT)
        BOTH = slice(0, NK + NT)
        ssq, var, tmp, rs = [sb(n, [P, NK + 2 * NT]) for n in ("ssq", "var", "tmp", "rs")]
        kn_hi = sb("kn_hi", [P, NT, 2 * C + 2], f32r)
        kn_lo = sb("kn_lo", [P, NT, 2 * C], f32r)
        q_hi, q_lo = sb("q_hi", [P, T], f32r), sb("q_lo", [P, T], f32r)
        k_tot = sb("k_tot", [P, 1])
        w1, w2, w3, w4, kvm = [sb(f"w{i}", [P, P]) for i in range(5)]
        m_t, m_b, tq = w1, w2, w3
        kvm_hi, kvm_lo = sb("kvm_hi", [P, P], f32r), sb("kvm_lo", [P, P], f32r)
        att_hi, att_lo = sb("att_hi", [P, T], f32r), sb("att_lo", [P, T], f32r)
        ffn_hi, ffn_lo = q_hi, q_lo
        xn_hi, xn_lo = sb("xn_hi", [P, T], f32r), sb("xn_lo", [P, T], f32r)

        th = sb("th", [P, NT, E])
        sig = sb("sig", [P, NT, E])
        score = sb("score", [P, NT, E])
        group = sb("group", [P, NT, NG + 4])
        group_top = sb("group_top", [P, NT, 8])
        group_left = sb("group_left", [P, NT, NG + 4])
        group_on = sb("group_on", [P, NT, NG])
        masked = sb("masked", [P, NT, E + 2])
        top = sb("top", [P, NT, 8])
        left = sb("left", [P, NT, E + 2])
        top_sum = sb("top_sum", [P, NT])
        top_eps = sb("top_eps", [P, NT])
        top_inv = sb("top_inv", [P, NT])
        picked = sig
        comb_tok = sb("comb_tok", [P, NT, 2, E])

        cur_hi, cur_lo = sb("cur_hi", [P, T], f32r), sb("cur_lo", [P, T], f32r)
        comb = sb("comb", [P, T])
        hid_hi = [sb(f"hid_hi{i}", [P, T], f32r) for i in range(R)]
        hid_lo = [sb(f"hid_lo{i}", [P, T], f32r) for i in range(R)]
        z = sb("z", [P, T])
        z_out = sb("z_out", [P, NT, C])

        gate_ps = [ps("gate_ps0"), ps("gate_ps1")]
        up_ps = [ps("up_ps0"), ps("up_ps1")]
        y_ps = ps("y_ps")
        A = [ps("a_ps0"), ps("a_ps1"), ps("a_ps2")]

        s_proj, s_cols, s_rows, s_x, s_store = [sem(n) for n in
                                                ("proj_in", "cols_in", "rows_in", "x_in", "stored")]
        s_stage = [sem(f"stage_in{i}") for i in range(3)]
        s_cent = sem("down_centred")
        s_mean = sem("down_mean")
        s_whi, s_wlo = sem("weights_hi"), sem("weights_lo")
        s_ones, s_mat, s_const = sem("ones_set"), sem("matrices_set"), sem("constants_set")
        s_setup = sem("setup_steps")
        s_b2 = sem("b2_centred")
        s_b2c = sem("b2c_copied")
        s_phi, s_plo, s_pc = sem("proj_hi_ready"), sem("proj_lo_ready"), sem("proj_centred")
        names = ("xhi xlo kvp kvb qp qhi qlo ksq ksum kn knhi knlo_p knlo_v ktv kt1 kt2 kt3 kt4 "
                 "ktot kvm kvmhi kvmlo attp att atthi attlo p1p ffn ffnhi ffnlo p2p cen cent csq "
                 "xntok xnt xnhi xnlo rtp th sig score gmax gtop gpad gleft gon mask ktop kpad tsum "
                 "teps tinv kleft pick combt combp comb curhi curlo "
                 "z zt zsq zout").split()
        s = {n: sem("s_" + n) for n in names}
        s_newton = sem("newton_steps")
        s_gate, s_up, s_silu, s_scaled, s_hid, s_hhi, s_hlo, s_down = [
            sem(n) for n in ("gate_ready", "up_ready", "silu_done", "scaled_done", "hid_done",
                             "hid_hi_done", "hid_lo_done", "down_done")]

        block = ctx.enter_context(nc.Block())

        def wait(eng, which, value):
            if not (isinstance(value, int) and value <= 0):
                eng.wait_ge(which, value)

        def chunks_done(b, step):
            return b * NS + (step + 1)

        NEWTON = 12

        def roots_done(call):
            return NEWTON * (call + 1)

        def scaled_done(b, step):
            return b * (NS - 1) + step

        @block.sync
        def _(sp):
            def load_x(n):
                wait(sp, s["att"], n)
                sp.dma_start(xt[:, :], x_t[n, :, :]).then_inc(s_x, 16)

            def store(b):
                sp.wait_ge(s["zout"], b + 1)
                sp.dma_start(out[b, :, :].rearrange("(t p) c -> p t c", p=P), z_out[:, :, :])\
                    .then_inc(s_store, 16)

            sp.dma_start(proj_f, proj).then_inc(s_proj, 16)
            sp.dma_start(xt[:, :], x_t[0, :, :]).then_inc(s_x, 16)
            for k in range(3 * SP3):
                m, part = k % 3, k // 3
                if k >= 3:
                    sp.wait_ge(s_wlo, k - 2)
                sp.dma_start(stage[k % 3],
                             moe_w[m, :, part * PC * P:(part + 1) * PC * P]
                             .rearrange("p (j h) -> p j h", j=PC)).then_inc(s_stage[k % 3], 16)
            load_x(1)
            with sp.Fori(1, NB - 1) as b:
                load_x(b + 1)
                store(b - 1)
            store(NB - 2)
            store(NB - 1)
            sp.wait_ge(s_store, 16 * NB)

        @block.tensor
        def _(pe):
            def three(out, w_hi, w_lo, m_hi, m_lo, start=True, stop=True):
                pe.matmul(out, w_hi, m_hi, start=start, stop=False)
                pe.matmul(out, w_hi, m_lo, start=False, stop=False)
                return pe.matmul(out, w_lo, m_hi, start=False, stop=stop)

            def weights(m, step):
                c = slice(step * P, (step + 1) * P)
                return moe_hi[m][:, c], moe_lo[m][:, c]

            def gate_up(b, step):
                if step == 0:
                    pe.wait_ge(s["curhi"], b + 1)
                    pe.wait_ge(s["curlo"], b + 1)
                    g, u = A[0], A[1]
                else:
                    g, u = gate_ps[(step - 1) % 2], up_ps[(step - 1) % 2]
                before = chunks_done(b, step - 2) if step >= 3 else chunks_done(b - 1, 30 + step)
                if step:
                    wait(pe, s_silu, before)
                three(g[:, :], *weights(0, step), cur_hi[:, :], cur_lo[:, :]).then_inc(s_gate, 1)
                if step:
                    wait(pe, s_hid, before)
                three(u[:, :], *weights(1, step), cur_hi[:, :], cur_lo[:, :]).then_inc(s_up, 1)

            def residual(b):
                wait(pe, s["z"], b)
                pe.matmul(y_ps[:, :], centre[:, :], cur_hi[:, :], start=True, stop=False)
                pe.matmul(y_ps[:, :], centre[:, :], cur_lo[:, :], start=False, stop=False)

            def down(b, step):
                pe.wait_ge(s_hhi, chunks_done(b, step))
                pe.wait_ge(s_hlo, chunks_done(b, step))
                last = three(y_ps[:, :], *weights(2, step), hid_hi[step % R][:, :],
                             hid_lo[step % R][:, :], start=False, stop=(step == NS - 1))
                last.then_inc(s_down, 1)

            def kv_proj(n, half):
                if half == 0:
                    pe.wait_ge(s["xhi"], n + 1)
                    pe.wait_ge(s["xlo"], n + 1)
                    wait(pe, s_hid, chunks_done(n - 1, 0))
                for t in range(2):
                    tok = slice((2 * half + t) * P, (2 * half + t + 1) * P)
                    o = A[half][:, t * 2 * C:(t + 1) * 2 * C]
                    w = slice(KO, KO + 2 * C)
                    pe.matmul(o, x_hi[:, tok], proj_hi[:, w], start=True, stop=False)
                    pe.matmul(o, x_lo[:, tok], proj_hi[:, w], start=False, stop=False)
                    last = pe.matmul(o, x_hi[:, tok], proj_lo[:, w], start=False, stop=True)
                last.then_inc(s["kvp"], 1)

            def q_proj(n):
                wait(pe, s["comb"], n)
                w = slice(QO, QO + C)
                three(A[2][:, :], proj_hi[:, w], proj_lo[:, w], x_hi[:, :], x_lo[:, :])\
                    .then_inc(s["qp"], 1)

            def k_t_v(n):
                pe.wait_ge(s["knhi"], 2 * n + 2)
                pe.wait_ge(s["knlo_p"], n + 1)
                pe.wait_ge(s["knlo_v"], n + 1)
                o = A[0][:, 0:C + 2]
                for t in range(NT):
                    k_h, k_l = kn_hi[:, t, 0:C], kn_lo[:, t, 0:C]
                    pe.matmul(o, k_h, kn_hi[:, t, C:2 * C + 2], start=(t == 0), stop=False)
                    pe.matmul(o, k_l, kn_hi[:, t, C:2 * C + 2], start=False, stop=False)
                    pe.matmul(A[0][:, 0:C], k_h, kn_lo[:, t, C:2 * C], start=False,
                              stop=(t == NT - 1))
                o = A[0][:, 2 * C:3 * C]
                for t in range(NT):
                    pe.matmul(o, ones_r[:, :], kn_hi[:, t, C:2 * C], start=(t == 0), stop=False)
                    last = pe.matmul(o, ones_r[:, :], kn_lo[:, t, C:2 * C], start=False,
                                     stop=(t == NT - 1))
                last.then_inc(s["ktv"], 1)

            def attend(n):
                for name in ("kvmhi", "kvmlo", "qhi", "qlo"):
                    pe.wait_ge(s[name], n + 1)
                three(A[1][:, :], kvm_hi[:, :], kvm_lo[:, :], q_hi[:, :], q_lo[:, :])\
                    .then_inc(s["attp"], 1)

            def project_1(n):
                pe.wait_ge(s["atthi"], n + 1)
                pe.wait_ge(s["attlo"], n + 1)
                wait(pe, s["zout"], n - 1)
                w = slice(P1O, P1O + C)
                three(A[2][:, :], proj_hi[:, w], proj_lo[:, w], att_hi[:, :], att_lo[:, :])\
                    .then_inc(s["p1p"], 1)

            def project_2(n):
                pe.matmul(A[0][:, :], centre2[:, :], x_hi[:, :], start=True, stop=False)
                pe.matmul(A[0][:, :], centre2[:, :], x_lo[:, :], start=False, stop=False)
                pe.wait_ge(s["ffnhi"], n + 1)
                pe.wait_ge(s["ffnlo"], n + 1)
                w = slice(P2O, P2O + C)
                three(A[0][:, :], proj_hi[:, w], proj_lo[:, w], ffn_hi[:, :], ffn_lo[:, :],
                      start=False).then_inc(s["p2p"], 1)

            def turn_cen(n):
                pe.wait_ge(s["cen"], n + 1)
                for k in range(NT):
                    tok = slice(k * P, (k + 1) * P)
                    last = pe.transpose(A[1][:, tok], cen[:, tok], ident[:, :])
                last.then_inc(s["cent"], 1)

            def turn_xn(n):
                pe.wait_ge(s["xntok"], n + 1)
                for k in range(NT):
                    last = pe.transpose(A[0][:, k * P:(k + 1) * P], xn_tok[:, k, :], ident[:, :])
                last.then_inc(s["xnt"], 1)

            def router(n):
                pe.wait_ge(s["xnhi"], n + 1)
                pe.wait_ge(s["xnlo"], n + 1)
                w = slice(GO, GO + E)
                for t in range(NT):
                    tok = slice(t * P, (t + 1) * P)
                    o = A[2][:, t * E:(t + 1) * E]
                    pe.matmul(o, xn_hi[:, tok], proj_hi[:, w], start=True, stop=False)
                    pe.matmul(o, xn_lo[:, tok], proj_hi[:, w], start=False, stop=False)
                    last = pe.matmul(o, xn_hi[:, tok], proj_lo[:, w], start=False, stop=True)
                last.then_inc(s["rtp"], 1)

            def turn_weights(n):
                pe.wait_ge(s["combt"], n + 1)
                for t in range(NT):
                    last = pe.transpose(A[2][:, t * P:(t + 1) * P],
                                        comb_tok[:, t, :, :].rearrange("p r e -> p (r e)"),
                                        ident[:, :])
                last.then_inc(s["combp"], 1)

            def turn_y(b):
                pe.wait_ge(s["z"], b + 1)
                for k in range(NT):
                    tok = slice(k * P, (k + 1) * P)
                    last = pe.transpose(A[2][:, tok], z[:, tok], ident[:, :])
                last.then_inc(s["zt"], 1)

            def batch(b, first, last):
                for step in range(NS):
                    gate_up(b, step)
                    if step == 0:
                        turn_weights(b)
                    if step == LAG:
                        residual(b)
                    if step >= LAG:
                        down(b, step - LAG)
                    elif not first:
                        down(b - 1, step - LAG + NS)
                    if not last:
                        if step == 2:
                            kv_proj(b + 1, 0)
                            q_proj(b + 1)
                        if step == 3:
                            kv_proj(b + 1, 1)
                    if step == 4 and not first:
                        pe.wait_ge(*((s["comb"], b + 1) if last else (s["qlo"], b + 2)))
                        turn_y(b - 1)
                    if not last:
                        if step == 11:
                            k_t_v(b + 1)
                        if step == 14:
                            attend(b + 1)
                        if step == 17:
                            project_1(b + 1)
                        if step == 21:
                            project_2(b + 1)
                        if step == 23:
                            turn_cen(b + 1)
                        if step == 26:
                            turn_xn(b + 1)
                        if step == 28:
                            router(b + 1)

            pe.wait_ge(s_mat, 1)
            pe.wait_ge(s_cols, 16)
            pe.matmul(A[2][:, 0:1], centre_f[:, :], b_2, start=True, stop=True).then_inc(s_b2, 1)
            pe.wait_ge(s_phi, 1)
            pe.wait_ge(s_plo, 1)
            kv_proj(0, 0)
            kv_proj(0, 1)
            pe.wait_ge(s_b2c, 1)
            q_proj(0)
            pe.wait_ge(s_const, 1)
            k_t_v(0)
            attend(0)
            project_1(0)
            project_2(0)
            turn_cen(0)
            turn_xn(0)
            router(0)
            pe.wait_ge(s_wlo, 3 * SP3)
            batch(0, True, False)
            with pe.Fori(1, NB - 1) as b:
                batch(b, False, False)
            batch(NB - 1, False, True)
            for step in range(NS - LAG, NS):
                down(NB - 1, step)
            turn_y(NB - 1)

        @block.scalar
        def _(act):
            def gate_act(b, step):
                act.wait_ge(s_gate, chunks_done(b, step))
                if step == R:
                    act.wait_ge(s_hid, chunks_done(b, 0))
                else:
                    wait(act, s_scaled, scaled_done(b, step - R) if step > R
                         else scaled_done(b - 1, step - R + NS))
                src = A[0] if step == 0 else gate_ps[(step - 1) % 2]
                act.activation(silu[step % R], src[:, :], ACT.Silu).then_inc(s_silu, 1)

            def hidden_hi(b, step):
                act.wait_ge(s_hid, chunks_done(b, step))
                wait(act, s_down, chunks_done(b, step - R))
                act.copy(hid_hi[step % R][:, :], hid[step % R]).then_inc(s_hhi, 1)

            def next_lo(n):
                wait(act, s_up, n * NS)
                act.wait_ge(s["xnlo"], n + 1)
                act.copy(cur_lo[:, :], xn_lo[:, :]).then_inc(s["curlo"], 1)

            def take_weights(n):
                act.wait_ge(s["combp"], n + 1)
                wait(act, s_scaled, scaled_done(n, 0))
                act.copy(comb[:, :], A[2][:, :]).then_inc(s["comb"], 1)

            def take_y(b):
                act.wait_ge(s_down, chunks_done(b, NS - 1))
                act.copy(z[:, :], y_ps[:, :]).then_inc(s["z"], 1)

            def square_y(b):
                wait(act, s_store, 16 * b)
                act.wait_ge(s["zt"], b + 1)
                for k in range(NT):
                    last = act.activation(z_out[:, k, :], A[2][:, k * P:(k + 1) * P], ACT.Square,
                                          accum_out=ssq[:, NK + k:NK + k + 1])
                last.then_inc(s["zsq"], 1)

            def norm_2(b, call):
                act.wait_ge(s_newton, roots_done(call))
                for k in range(NT):
                    last = act.activation(z_out[:, k, :], A[2][:, k * P:(k + 1) * P], ACT.Copy,
                                          scale=rs[:, NK + k:NK + k + 1])
                last.then_inc(s["zout"], 1)

            def split_x(n):
                act.wait_ge(s_x, 16 * n + 16)
                wait(act, s["p2p"], n)
                act.copy(x_hi[:, :], xt[:, :]).then_inc(s["xhi"], 1)

            def split_q(n):
                act.wait_ge(s["qp"], n + 1)
                act.activation(q_hi[:, :], A[2][:, :], ACT.Identity, bias=b_q).then_inc(s["qhi"], 1)

            def square_kv(n, half):
                act.wait_ge(s["kvb"], 2 * n + half + 1)
                t = slice(2 * half, 2 * half + 2)
                act.activation(kv_sq[:, t, :], kv[:, t, :], ACT.Square).then_inc(s["ksq"], 1)

            def split_kn(n, half):
                act.wait_ge(s["kn"], 2 * n + half + 1)
                t = slice(2 * half, 2 * half + 2)
                act.copy(kn_hi[:, t, 0:2 * C], kv[:, t, :]).then_inc(s["knhi"], 1)

            def split_kvm(n):
                act.wait_ge(s["kvm"], n + 1)
                act.copy(kvm_hi[:, :], kvm[:, :]).then_inc(s["kvmhi"], 1)

            def split_att(n):
                act.wait_ge(s["att"], n + 1)
                act.copy(att_hi[:, :], att).then_inc(s["atthi"], 1)

            def gelu(n):
                act.wait_ge(s["p1p"], n + 1)
                act.activation(ffn_hi[:, :], A[2][:, :], ACT.Gelu, bias=b_1).then_inc(s["ffnhi"], 1)
                act.activation(ffn, A[2][:, :], ACT.Gelu, bias=b_1).then_inc(s["ffn"], 1)

            def take_cen(n):
                act.wait_ge(s["p2p"], n + 1)
                act.activation(cen, A[0][:, :], ACT.Identity, bias=b_2c[:, :])\
                    .then_inc(s["cen"], 1)

            def square_cen(n):
                act.wait_ge(s["cent"], n + 1)
                for k in range(NT):
                    c = NK + NT + k
                    last = act.activation(xn_tok[:, k, :], A[1][:, k * P:(k + 1) * P], ACT.Square,
                                          accum_out=ssq[:, c:c + 1])
                last.then_inc(s["csq"], 1)

            def norm_1(n):
                act.wait_ge(s_newton, roots_done(2 * n + 1))
                for k in range(NT):
                    c = NK + NT + k
                    last = act.activation(xn_tok[:, k, :], A[1][:, k * P:(k + 1) * P], ACT.Copy,
                                          scale=rs[:, c:c + 1])
                last.then_inc(s["xntok"], 1)

            def split_xn(n):
                act.wait_ge(s["xnt"], n + 1)
                act.copy(xn_hi[:, :], A[0][:, :]).then_inc(s["xnhi"], 1)

            def tanh(n):
                act.wait_ge(s["rtp"], n + 1)
                act.activation(th[:, :, :], A[2][:, 0:NT * E].rearrange("p (t e) -> p t e", t=NT),
                               ACT.Tanh, scale=0.5).then_inc(s["th"], 1)

            def batch(b, first, last):
                for step in range(NS):
                    if step == 0 and not last:
                        split_x(b + 1)
                    if step == 1:
                        take_weights(b)
                    if step == LAG and not first:
                        take_y(b - 1)
                    gate_act(b, step)
                    if step == NS - 1 and not last:
                        next_lo(b + 1)
                    if step >= 1:
                        hidden_hi(b, step - 1)
                    elif not first:
                        hidden_hi(b - 1, NS - 1)
                    if step == 5 and not first:
                        square_y(b - 1)
                    if step == 7 and not first:
                        norm_2(b - 1, 2 * (b + 1))
                    if not last:
                        if step == 3:
                            split_q(b + 1)
                            square_kv(b + 1, 0)
                        if step == 4:
                            square_kv(b + 1, 1)
                        if step == 7:
                            split_kn(b + 1, 0)
                        if step == 8:
                            split_kn(b + 1, 1)
                        if step == 12:
                            split_kvm(b + 1)
                        if step == 15:
                            split_att(b + 1)
                        if step == 18:
                            gelu(b + 1)
                        if step == 22:
                            take_cen(b + 1)
                        if step == 24:
                            square_cen(b + 1)
                        if step == 25:
                            norm_1(b + 1)
                        if step == 27:
                            split_xn(b + 1)
                        if step == 29:
                            tanh(b + 1)

            def split_piece(k):
                m, part = k % 3, k // 3
                if m == 2:
                    act.wait_ge(s_cent, part + 1)
                else:
                    act.wait_ge(s_stage[k % 3], 16 * (part + 1))
                act.copy(moe_hi[m][:, part * PC * P:(part + 1) * PC * P],
                         stage[k % 3].rearrange("p j h -> p (j h)")).then_inc(s_whi, 1)

            act.dma_start(col[:, :], cols).then_inc(s_cols, 16)
            act.dma_start(row[:, :], rows.partition_broadcast(P)).then_inc(s_rows, 16)
            split_x(0)
            act.wait_ge(s_pc, 2)
            act.copy(proj_hi[:, :], proj_f).then_inc(s_phi, 1)
            split_piece(0)
            split_q(0)
            square_kv(0, 0)
            square_kv(0, 1)
            split_piece(1)
            split_kn(0, 0)
            split_kn(0, 1)
            split_piece(2)
            split_piece(3)
            split_kvm(0)
            split_piece(4)
            split_att(0)
            split_piece(5)
            gelu(0)
            act.wait_ge(s_b2c, 1)
            take_cen(0)
            split_piece(6)
            square_cen(0)
            split_piece(7)
            norm_1(0)
            split_xn(0)
            split_piece(8)
            tanh(0)
            next_lo(0)
            batch(0, True, False)
            with act.Fori(1, NB - 1) as b:
                batch(b, False, False)
            batch(NB - 1, False, True)
            hidden_hi(NB - 1, NS - 1)
            take_y(NB - 1)
            square_y(NB - 1)
            norm_2(NB - 1, 2 * NB + 1)

        @block.gpsimd
        def _(pool):
            def scale(b, step):
                pool.wait_ge(s_silu, chunks_done(b, step))
                if step == 1:
                    pool.wait_ge(s["comb"], b + 1)
                wait(pool, s_hid, chunks_done(b, step - R))
                pool.tensor_tensor(scaled[step % R], silu[step % R], comb[:, :],
                                   ALU.mult).then_inc(s_scaled, 1)

            def rest(out, whole, hi, done):
                pool.tensor_tensor(out, whole, hi, ALU.subtract).then_inc(done, 1)

            def rest_kn(n):
                pool.wait_ge(s["knhi"], 2 * n + 1)
                rest(kn_lo[:, 0:2, :], kv[:, 0:2, :], kn_hi[:, 0:2, 0:2 * C], s["knlo_p"])

            def rest_att(n):
                pool.wait_ge(s["atthi"], n + 1)
                rest(att_lo[:, :], att, att_hi[:, :], s["attlo"])

            def rest_ffn(n):
                pool.wait_ge(s["ffnhi"], n + 1)
                pool.wait_ge(s["ffn"], n + 1)
                rest(ffn_lo[:, :], ffn, ffn_hi[:, :], s["ffnlo"])

            def batch(b, first, last):
                for step in range(NS):
                    if step >= 1:
                        scale(b, step)
                    if not last:
                        if step == 8:
                            rest_kn(b + 1)
                        if step == 15:
                            rest_att(b + 1)
                        if step == 19:
                            rest_ffn(b + 1)

            def rest_piece(k):
                m, part = k % 3, k // 3
                pool.wait_ge(s_whi, k + 1)
                wait(pool, s_wlo, k)
                rest(moe_lo[m][:, part * PC * P:(part + 1) * PC * P],
                     stage[k % 3].rearrange("p j h -> p (j h)"),
                     moe_hi[m][:, part * PC * P:(part + 1) * PC * P], s_wlo)

            pool.memset(ones_f[:, :], 1.0).then_inc(s_ones, 1)
            pool.memset(centre_f[:, :], -1.0 / P).then_inc(s_ones, 1)
            pool.memset(ident[:, :], 0.0).then_inc(s_ones, 1)
            pool.memset(blocks[:, :, :], 1.0).then_inc(s_ones, 1)
            pool.memset(kn_hi[:, :, 2 * C:2 * C + 2].bitcast(fp32), 1.0).then_inc(s_ones, 1)
            pool.memset(group[:, :, NG:NG + 4], PAD).then_inc(s_ones, 1)
            pool.memset(masked[:, :, E:E + 2], PAD).then_inc(s_ones, 1)
            pool.wait_ge(s_ones, 7)
            pool.affine_select(out=centre_f[:, :], in_=centre_f[:, :], compare_op=ALU.not_equal,
                               fill=1.0 - 1.0 / P, base=0, pattern=[[-1, P]],
                               channel_multiplier=1).then_inc(s_mat, 1)
            pool.affine_select(out=ident[:, :], in_=ident[:, :], compare_op=ALU.not_equal,
                               fill=1.0, base=0, pattern=[[-1, P]],
                               channel_multiplier=1).then_inc(s_mat, 1)
            pool.affine_select(out=blocks[:, :, :], in_=blocks[:, :, :], compare_op=ALU.is_ge,
                               fill=0.0, base=0, pattern=[[-HD, NH], [0, HD]],
                               channel_multiplier=1).then_inc(s_mat, 1)
            pool.wait_ge(s_mat, 3)
            pool.affine_select(out=blocks[:, :, :], in_=blocks[:, :, :], compare_op=ALU.is_ge,
                               fill=0.0, base=HD - 1, pattern=[[HD, NH], [0, HD]],
                               channel_multiplier=-1).then_inc(s_mat, 1)
            rest_piece(0)
            rest_piece(1)
            rest_kn(0)
            rest_piece(2)
            rest_piece(3)
            rest_att(0)
            rest_piece(4)
            rest_piece(5)
            rest_ffn(0)
            rest_piece(6)
            rest_piece(7)
            rest_piece(8)
            batch(0, True, False)
            with pool.Fori(1, NB - 1) as b:
                batch(b, False, False)
            batch(NB - 1, False, True)

        @block.vector
        def _(dve):
            def product(b, step):
                if step == 0:
                    dve.wait_ge(s_silu, chunks_done(b, 0))
                    gate, up = silu[0], A[1]
                else:
                    dve.wait_ge(s_scaled, scaled_done(b, step))
                    gate, up = scaled[step % R], up_ps[(step - 1) % 2]
                dve.wait_ge(s_up, chunks_done(b, step))
                wait(dve, s_hlo, chunks_done(b, step - R))
                dve.tensor_tensor(hid[step % R], gate[:, :], up[:, :], ALU.mult)\
                    .then_inc(s_hid, 1)

            def hidden_lo(b, step):
                dve.wait_ge(s_hhi, chunks_done(b, step))
                dve.tensor_tensor(hid_lo[step % R][:, :], hid[step % R],
                                  hid_hi[step % R][:, :], ALU.subtract).then_inc(s_hlo, 1)

            def next_hi(n):
                wait(dve, s_up, n * NS)
                dve.wait_ge(s["xnhi"], n + 1)
                dve.tensor_copy(cur_hi[:, :], xn_hi[:, :]).then_inc(s["curhi"], 1)

            def rest_x(n):
                dve.wait_ge(s["xhi"], n + 1)
                dve.tensor_tensor(x_lo[:, :], xt[:, :], x_hi[:, :], ALU.subtract)\
                    .then_inc(s["xlo"], 1)

            def add_bias(n, half):
                dve.wait_ge(s["kvp"], 2 * n + half + 1)
                t = slice(2 * half, 2 * half + 2)
                dve.tensor_tensor(kv[:, t, :], A[half][:, :].rearrange("p (t c) -> p t c", t=2),
                                  b_kv.unsqueeze(1).to_broadcast([P, 2, 2 * C]), ALU.add)\
                    .then_inc(s["kvb"], 1)

            def rest_q(n):
                dve.wait_ge(s["qhi"], n + 1)
                dve.scalar_tensor_tensor(q_lo[:, :], A[2][:, :], b_q, q_hi[:, :], ALU.add,
                                         ALU.subtract).then_inc(s["qlo"], 1)

            def sum_squares(n, half):
                dve.wait_ge(s["ksq"], 2 * n + half + 1)
                t = slice(2 * half, 2 * half + 2)
                dve.tensor_reduce(ssq[:, 4 * half * NH:4 * (half + 1) * NH],
                                  kv_sq[:, t, :].rearrange("p t (g d) -> p (t g) d", d=HD),
                                  AX.X, ALU.add).then_inc(s["ksum"], 1)

            def rsqrt(call, c, means):
                def then(step, instruction):
                    instruction.then_inc(s_newton, 1)
                    dve.wait_ge(s_newton, call * NEWTON + step)

                for cols_of, size in means:
                    last = dve.tensor_scalar(var[:, cols_of], ssq[:, cols_of], 1.0 / size, EPS,
                                             ALU.mult, ALU.add)
                then(1, last)
                then(2, dve.tensor_scalar(tmp[:, c].bitcast(i32), var[:, c].bitcast(i32), 1, None,
                                          ALU.logical_shift_right))
                then(3, dve.tensor_scalar(rs[:, c].bitcast(i32), tmp[:, c].bitcast(i32), -1.0,
                                          float(0x5f3759df), ALU.mult, ALU.add))
                for k in range(3):
                    then(4 + 3 * k, dve.scalar_tensor_tensor(tmp[:, c], rs[:, c], -0.5, rs[:, c],
                                                             ALU.mult, ALU.mult))
                    then(5 + 3 * k, dve.tensor_tensor(tmp[:, c], tmp[:, c], var[:, c], ALU.mult))
                    then(6 + 3 * k, dve.scalar_tensor_tensor(rs[:, c], tmp[:, c], 1.5, rs[:, c],
                                                             ALU.add, ALU.mult))

            def kv_rstds(n, with_ln2):
                dve.wait_ge(s["ksum"], 2 * n + 2)
                if with_ln2:
                    dve.wait_ge(s["zsq"], n - 1)
                rsqrt(2 * n, BOTH if with_ln2 else KV, [(KV, HD)] + [(LN2, C)] * with_ln2)

            def ln2_rstds(b, call):
                dve.wait_ge(s["zsq"], b + 1)
                rsqrt(call, LN2, [(LN2, C)])

            def ln1_rstds(n):
                dve.wait_ge(s["csq"], n + 1)
                rsqrt(2 * n + 1, LN1, [(LN1, C)])

            def normalise_kv(n, half):
                dve.wait_ge(s_newton, roots_done(2 * n))
                t = slice(2 * half, 2 * half + 2)
                view = kv[:, t, :].rearrange("p t (g d) -> p (t g) d", d=HD)
                r = rs[:, 4 * half * NH:4 * (half + 1) * NH].unsqueeze(2)
                dve.tensor_tensor(view, view, r.to_broadcast([P, 4 * NH, HD]), ALU.mult)\
                    .then_inc(s["kn"], 1)

            def rest_kn(n):
                dve.wait_ge(s["knhi"], 2 * n + 2)
                dve.tensor_tensor(kn_lo[:, 2:4, :], kv[:, 2:4, :], kn_hi[:, 2:4, 0:2 * C],
                                  ALU.subtract).then_inc(s["knlo_v"], 1)

            def scale_ktv(n):
                dve.wait_ge(s["ktv"], n + 1)
                dve.tensor_copy(k_tot[:, :], A[0][:, C:C + 1]).then_inc(s["ktot"], 1)
                dve.tensor_tensor(w1[:, :], A[0][:, 0:C], m_kv[:, :], ALU.mult)\
                    .then_inc(s["kt1"], 1)
                dve.tensor_tensor(w3[:, :], A[0][:, 2 * C:3 * C], m_v[:, :], ALU.mult)\
                    .then_inc(s["kt3"], 1)
                dve.wait_ge(s["ktot"], n + 1)
                dve.wait_ge(s["kt1"], n + 1)
                dve.scalar_tensor_tensor(w2[:, :], m_k[:, :], k_tot[:, :], w1[:, :], ALU.mult,
                                         ALU.add).then_inc(s["kt2"], 1)

            def add_ktv(n):
                dve.wait_ge(s["kt3"], n + 1)
                dve.tensor_tensor(w4[:, :], w3[:, :], m_1[:, :], ALU.add).then_inc(s["kt4"], 1)
                dve.wait_ge(s["kt2"], n + 1)
                dve.wait_ge(s["kt4"], n + 1)
                dve.tensor_tensor(kvm[:, :], w4[:, :], w2[:, :], ALU.add).then_inc(s["kvm"], 1)

            def rest_kvm(n):
                dve.wait_ge(s["kvmhi"], n + 1)
                dve.tensor_tensor(kvm_lo[:, :], kvm[:, :], kvm_hi[:, :], ALU.subtract)\
                    .then_inc(s["kvmlo"], 1)

            def add_x(n):
                dve.wait_ge(s["attp"], n + 1)
                dve.tensor_tensor(att, xt[:, :], A[1][:, :], ALU.add).then_inc(s["att"], 1)

            def rest_xn(n):
                dve.wait_ge(s["xnhi"], n + 1)
                dve.tensor_tensor(xn_lo[:, :], A[0][:, :], xn_hi[:, :], ALU.subtract)\
                    .then_inc(s["xnlo"], 1)

            def hold(which, value):
                dve.wait_ge(which, value)
                dve.memset(held[:, :], 0.0)

            def scores(n):
                dve.wait_ge(s["th"], n + 1)
                dve.tensor_scalar(sig[:, :, :], th[:, :, :], 0.5, 0.5, ALU.mult, ALU.add)\
                    .then_inc(s["sig"], 1)
                dve.wait_ge(s["sig"], n + 1)
                dve.tensor_tensor(score[:, :, :], sig[:, :, :],
                                  b_gate.unsqueeze(1).to_broadcast([P, NT, E]), ALU.add)\
                    .then_inc(s["score"], 1)
                dve.wait_ge(s["score"], n + 1)
                dve.tensor_reduce(group[:, :, 0:NG],
                                  score[:, :, :].rearrange("p t (g e) -> p t g e", g=NG),
                                  AX.X, ALU.max).then_inc(s["gmax"], 1)

            def pick_groups(n):
                hold(s["gmax"], n + 1)
                for t in range(NT):
                    last = dve.max(group_top[:, t, :], group[:, t, 0:NG])
                last.then_inc(s["gtop"], 1)
                dve.wait_ge(s["gtop"], n + 1)
                dve.memset(group_top[:, :, TOPG:8], PAD).then_inc(s["gpad"], 1)
                hold(s["gpad"], n + 1)
                for t in range(NT):
                    last = dve.match_replace(group_left[:, t, :], group_top[:, t, :],
                                             group[:, t, :], -PAD)
                last.then_inc(s["gleft"], 1)
                dve.wait_ge(s["gleft"], n + 1)
                dve.tensor_tensor(group_on[:, :, :], group[:, :, 0:NG], group_left[:, :, 0:NG],
                                  ALU.not_equal).then_inc(s["gon"], 1)

            def pick_experts(n):
                dve.wait_ge(s["gon"], n + 1)
                for t in range(NT):
                    last = dve.tensor_tensor(
                        masked[:, t, 0:E].rearrange("p (g e) -> p g e", g=NG),
                        score[:, t, :].rearrange("p (g e) -> p g e", g=NG),
                        group_on[:, t, :].unsqueeze(2).to_broadcast([P, NG, EG]), ALU.mult)
                last.then_inc(s["mask"], 1)
                hold(s["mask"], n + 1)
                for t in range(NT):
                    last = dve.max(top[:, t, :], masked[:, t, 0:E])
                last.then_inc(s["ktop"], 1)
                dve.wait_ge(s["ktop"], n + 1)
                dve.tensor_reduce(top_sum[:, :], top[:, :, 0:TOPK], AX.X, ALU.add)\
                    .then_inc(s["tsum"], 1)
                dve.memset(top[:, :, TOPK:8], PAD).then_inc(s["kpad"], 1)

            def weigh(n):
                hold(s["kpad"], n + 1)
                for t in range(NT):
                    last = dve.match_replace(left[:, t, :], top[:, t, :], masked[:, t, :], 0.0)
                last.then_inc(s["kleft"], 1)
                dve.wait_ge(s["tsum"], n + 1)
                dve.tensor_scalar(top_eps[:, :], top_sum[:, :], 1e-8, None, ALU.add)\
                    .then_inc(s["teps"], 1)
                dve.wait_ge(s["teps"], n + 1)
                dve.reciprocal(top_inv[:, :], top_eps[:, :]).then_inc(s["tinv"], 1)
                dve.wait_ge(s["kleft"], n + 1)
                dve.tensor_tensor(picked[:, :, :], masked[:, :, 0:E], left[:, :, 0:E],
                                  ALU.subtract).then_inc(s["pick"], 1)
                dve.wait_ge(s["pick"], n + 1)
                dve.wait_ge(s["tinv"], n + 1)
                wait(dve, s["combp"], n)
                for r in range(2):
                    last = dve.tensor_tensor(comb_tok[:, :, r, :], picked[:, :, :],
                                             top_inv[:, :].unsqueeze(2).to_broadcast([P, NT, E]),
                                             ALU.mult)
                last.then_inc(s["combt"], 1)

            def batch(b, first, last):
                for step in range(NS):
                    if step == 0 and not last:
                        rest_x(b + 1)
                    if step == NS - 1 and not last:
                        next_hi(b + 1)
                    if step >= 1:
                        hidden_lo(b, step - 1)
                    elif not first:
                        hidden_lo(b - 1, NS - 1)
                    product(b, step)
                    if not last:
                        if step == 2:
                            add_bias(b + 1, 0)
                        if step == 3:
                            add_bias(b + 1, 1)
                            rest_q(b + 1)
                        if step == 4:
                            sum_squares(b + 1, 0)
                        if step == 5:
                            sum_squares(b + 1, 1)
                            kv_rstds(b + 1, not first)
                        if step == 6:
                            normalise_kv(b + 1, 0)
                        if step == 7:
                            normalise_kv(b + 1, 1)
                        if step == 8:
                            rest_kn(b + 1)
                    if step == 5 and last:
                        ln2_rstds(b - 1, 2 * (b + 1))
                    if not last:
                        if step == 11:
                            scale_ktv(b + 1)
                            add_ktv(b + 1)
                        if step == 12:
                            rest_kvm(b + 1)
                        if step == 14:
                            add_x(b + 1)
                        if step == 24:
                            ln1_rstds(b + 1)
                        if step == 27:
                            rest_xn(b + 1)
                        if step == 29:
                            scores(b + 1)
                        if step == 30:
                            pick_groups(b + 1)
                        if step == 31:
                            pick_experts(b + 1)
                        if step == 32:
                            weigh(b + 1)

            setup = [0]

            def chained(instruction):
                setup[0] += 1
                instruction.then_inc(s_setup, 1)
                dve.wait_ge(s_setup, setup[0])

            def centre_piece(part):
                dve.wait_ge(s_stage[2], 16 * (part + 1))
                dve.tensor_reduce(stage_mean[:, :], stage[2], AX.X, ALU.add)\
                    .then_inc(s_mean, 1)
                dve.wait_ge(s_mean, part + 1)
                dve.scalar_tensor_tensor(stage[2],
                                         stage_mean[:, :].unsqueeze(2).to_broadcast([P, PC, P]),
                                         -1.0 / P, stage[2], ALU.mult, ALU.add)\
                    .then_inc(s_cent, 1)

            w_kv = proj_f[:, KO:KO + 2 * C].rearrange("p (g d) -> p g d", d=HD)
            w_p2 = proj_f[:, P2O:P2O + C]
            dve.wait_ge(s_proj, 16)
            chained(dve.tensor_reduce(mean_kv[:, :], w_kv, AX.X, ALU.add))
            dve.scalar_tensor_tensor(w_kv, mean_kv[:, :].unsqueeze(2).to_broadcast([P, 2 * NH, HD]),
                                     -1.0 / HD, w_kv, ALU.mult, ALU.add).then_inc(s_pc, 1)
            chained(dve.tensor_reduce(mean_p2[:, :], w_p2, AX.X, ALU.add))
            chained(dve.tensor_scalar(neg_p2[:, :], mean_p2[:, :], -1.0 / C, None, ALU.mult))
            dve.tensor_scalar(w_p2, w_p2, neg_p2[:, :], None, ALU.add).then_inc(s_pc, 1)
            rest_x(0)
            dve.wait_ge(s_phi, 1)
            dve.tensor_tensor(proj_lo[:, :], proj_f, proj_hi[:, :], ALU.subtract)\
                .then_inc(s_plo, 1)
            dve.wait_ge(s_rows, 16)
            bias_kv = b_kv.rearrange("p (g d) -> p g d", d=HD)
            chained(dve.tensor_reduce(mean_b[:, :], bias_kv, AX.X, ALU.add))
            chained(dve.scalar_tensor_tensor(
                bias_kv, mean_b[:, :].unsqueeze(2).to_broadcast([P, 2 * NH, HD]), -1.0 / HD,
                bias_kv, ALU.mult, ALU.add))
            dve.wait_ge(s_b2, 1)
            dve.tensor_copy(b_2c[:, :], A[2][:, 0:1]).then_inc(s_b2c, 1)
            add_bias(0, 0)
            add_bias(0, 1)
            rest_q(0)
            sum_squares(0, 0)
            sum_squares(0, 1)
            kv_rstds(0, False)
            normalise_kv(0, 0)
            normalise_kv(0, 1)
            dve.wait_ge(s_mat, 4)
            dve.tensor_copy(centre[:, :], centre_f[:, :])
            dve.tensor_scalar(centre2[:, :], centre_f[:, :], 2.0, None, ALU.mult)
            dve.tensor_copy(ones_r[:, :], ones_f[:, :]).then_inc(s_const, 1)
            rest_kn(0)
            centre_piece(0)
            flat = blocks[:, :, :].rearrange("p h d -> p (h d)")
            dve.wait_ge(s_cols, 16)
            chained(dve.tensor_scalar(tq[:, :], flat, temp, 1.0 / T, ALU.mult, ALU.mult))
            dve.scalar_tensor_tensor(m_kv[:, :], tq[:, :], g_k, g_v, ALU.mult, ALU.mult)
            dve.scalar_tensor_tensor(m_k[:, :], tq[:, :], g_k, b_v, ALU.mult, ALU.mult)
            dve.scalar_tensor_tensor(m_v[:, :], tq[:, :], b_k, g_v, ALU.mult, ALU.mult)
            dve.scalar_tensor_tensor(m_t[:, :], tq[:, :], b_k, b_v, ALU.mult, ALU.mult)
            chained(dve.tensor_tensor(m_b[:, :].rearrange("p (h d) -> p h d", d=HD),
                                      blocks[:, :, :],
                                      att_bias.unsqueeze(1).to_broadcast([P, NH, HD]), ALU.mult))
            chained(dve.scalar_tensor_tensor(m_1[:, :], m_t[:, :], float(T), m_b[:, :], ALU.mult,
                                             ALU.add))
            scale_ktv(0)
            add_ktv(0)
            rest_kvm(0)
            add_x(0)
            centre_piece(1)
            ln1_rstds(0)
            centre_piece(2)
            rest_xn(0)
            next_hi(0)
            scores(0)
            pick_groups(0)
            pick_experts(0)
            weigh(0)
            batch(0, True, False)
            with dve.Fori(1, NB - 1) as b:
                batch(b, False, False)
            batch(NB - 1, False, True)
            hidden_lo(NB - 1, NS - 1)
            ln2_rstds(NB - 1, 2 * NB + 1)


def kernel(**inputs):
    import numpy as np
    import concourse.bacc as bacc
    from concourse import mybir as mb
    from concourse.bass_utils import run_bass_kernel_spmd

    a = {k: np.asarray(v) for k, v in inputs.items()}
    x = a["L0_attn_x"]
    nb, t, c = x.shape
    heads = a["L0_attn_temperature"].shape[0]
    hd = c // heads
    wt = a["L0_attn_qkv_w"].T

    def units(w, k):
        e, i = w.shape[:2]
        return w.reshape(e, i // k, k, *w.shape[2:]).transpose(1, 2, 0, 3)

    def per_unit(w, shared):
        routed = units(w, 2)
        return np.concatenate([shared.T, routed.reshape(-1, c).T], axis=1)

    down = units(a["L0_ffn_ed_w"].transpose(0, 2, 1), 2)
    down = down.reshape(down.shape[0], -1, c).transpose(1, 0, 2).reshape(c, -1)
    layout = {
        "x_t": x.transpose(0, 2, 1),
        "proj": np.concatenate([wt, a["L0_attn_p1_w"].T, a["L0_attn_p2_w"].T,
                                a["L0_ffn_gate_w"].T], axis=1),
        "cols": np.concatenate([v.reshape(c, -1) for v in (
            a["L0_attn_qkv_b"][:c], a["L0_attn_p1_b"], a["L0_attn_p2_b"],
            np.repeat(a["L0_attn_temperature"].reshape(-1), hd),
            np.tile(a["L0_attn_kn_g"], heads), np.tile(a["L0_attn_kn_b"], heads),
            a["L0_attn_attn_bias"])], axis=1),
        "rows": np.concatenate([a["L0_attn_qkv_b"][c:], np.tile(a["L0_attn_vn_g"], heads),
                                np.tile(a["L0_attn_vn_b"], heads), a["L0_ffn_gate_bias"]]),
        "moe_w": np.stack([per_unit(a["L0_ffn_eg_w"], a["L0_ffn_sg_w"]),
                           per_unit(a["L0_ffn_eu_w"], a["L0_ffn_su_w"]),
                           np.concatenate([a["L0_ffn_sd_w"].T, down], axis=1)]),
    }
    nc = bacc.Bacc("TRN2", target_bir_lowering=False, num_devices=1)
    arrays, args = {}, []
    for name, v in layout.items():
        v = np.ascontiguousarray(v)
        arrays[name + "_in"] = v
        args.append(nc.dram_tensor(name + "_in", v.shape, mb.dt.from_np(v.dtype),
                                   kind="ExternalInput").ap())
    args.append(nc.dram_tensor("out", (nb, t, c), mb.dt.from_np(x.dtype),
                               kind="ExternalOutput").ap())
    post_ln_block(nc, *args)
    r = run_bass_kernel_spmd(nc, [arrays], core_ids=[0])
    return r.results[0]["out"]
```

```python
from contextlib import ExitStack

import concourse.bass as bass
from concourse import mybir


def post_ln_block(
    nc: bass.Bass,
    x_t: bass.AP,
    proj: bass.AP,
    cols: bass.AP,
    rows: bass.AP,
    moe_w: bass.AP,
    out: bass.AP,
):
    fp32 = mybir.dt.float32
    f32r = mybir.dt.float32r
    i32 = mybir.dt.int32
    ALU = mybir.AluOpType
    ACT = mybir.ActivationFunctionType
    AX = mybir.AxisListType

    NB, C, T = x_t.shape
    P = 128
    HD = 8
    NH = C // HD
    NT = T // P
    E = 64
    NG, TOPG, TOPK = 8, 4, 6
    EG = E // NG
    NS = moe_w.shape[2] // P
    SP3 = 3
    PC = NS // SP3
    EPS = 1e-5
    PAD = -3.0e38
    LAG = 3
    R = 3

    ctx = ExitStack()
    with ctx:
        def sb(name, shape, dt=fp32):
            return ctx.enter_context(nc.sbuf_tensor(name, shape, dt))

        def ps(name):
            return ctx.enter_context(nc.psum_tensor(name, [P, T], fp32))

        def sem(name):
            return ctx.enter_context(nc.semaphore(name))

        moe_hi = [sb(f"moe_hi{m}", [P, NS * P], f32r) for m in range(3)]
        moe_lo = [sb(f"moe_lo{m}", [P, NS * P], f32r) for m in range(3)]
        work = sb("work", [P, 3 * R, T])
        silu = [work[:, i, :] for i in range(R)]
        scaled = [work[:, R + i, :] for i in range(R)]
        hid = [work[:, 2 * R + i, :] for i in range(R)]
        stage = [work[:, 3 * i:3 * i + 3, :].rearrange("p a t -> p (a t)")[:, 0:PC * P]
                 .rearrange("p (j h) -> p j h", h=P) for i in range(3)]
        stage_mean = sb("stage_mean", [P, PC])
        PW = proj.shape[1]
        QO, KO, P1O, P2O, GO = 0, C, 3 * C, 4 * C, 5 * C
        shared = sb("shared", [P, 2 * T])
        proj_f = shared[:, 0:PW]
        kv_sq = shared[:, :].rearrange("p (t c) -> p t c", c=2 * C)
        att, ffn = shared[:, 0:T], shared[:, T:2 * T]
        proj_hi = sb("proj_hi", [P, PW], f32r)
        proj_lo = sb("proj_lo", [P, PW], f32r)
        col = sb("col", [P, cols.shape[1]])
        b_q, b_1, b_2, temp, g_k, b_k = [col[:, i:i + 1] for i in range(6)]
        att_bias = col[:, 6:6 + HD]
        row = sb("row", [P, rows.shape[0]])
        b_kv = row[:, 0:2 * C]
        g_v, b_v = row[:, 2 * C:3 * C], row[:, 3 * C:4 * C]
        b_gate = row[:, 4 * C:4 * C + E]
        mean_kv = sb("mean_kv", [P, 2 * NH])
        mean_b = sb("mean_b", [P, 2 * NH])
        mean_p2 = sb("mean_p2", [P, 1])
        neg_p2 = sb("neg_p2", [P, 1])
        b_2c = sb("b_2c", [P, 1])

        ident = sb("ident", [P, P])
        centre_f = sb("centre_f", [P, P])
        centre = sb("centre", [P, P], f32r)
        centre2 = sb("centre2", [P, P], f32r)
        ones_f = sb("ones_f", [P, P])
        ones_r = sb("ones_r", [P, P], f32r)
        blocks = sb("blocks", [P, NH, HD])
        m_kv, m_k, m_v, m_1 = [sb(f"m_{i}", [P, P]) for i in range(4)]

        xt = sb("xt", [P, T])
        x_hi, x_lo = sb("x_hi", [P, T], f32r), sb("x_lo", [P, T], f32r)
        kv_room = sb("kv_room", [P, NT * 2 * C])
        kv = kv_room[:, :].rearrange("p (t c) -> p t c", c=2 * C)
        cen = kv_room[:, 0:T]
        xn_tok = kv_room[:, T:2 * T].rearrange("p (t c) -> p t c", c=C)
        held = sb("held", [P, 1])
        NK = NT * 2 * NH
        KV, LN2, LN1 = slice(0, NK), slice(NK, NK + NT), slice(NK + NT, NK + 2 * NT)
        LNS = slice(NK, NK + 2 * NT)
        ssq, var, tmp, rs = [sb(n, [P, NK + 2 * NT]) for n in ("ssq", "var", "tmp", "rs")]
        kn = sb("kn", [P, NT, 4 * C + 4], f32r)
        K_HI, K_LO, ONES = slice(0, C), slice(C, 2 * C), slice(2 * C, 2 * C + 2)
        V = slice(2 * C + 2, 4 * C + 2)
        q_hi, q_lo = sb("q_hi", [P, T], f32r), sb("q_lo", [P, T], f32r)
        k_tot = sb("k_tot", [P, 1])
        w1, w2, w3, kvm = [sb(f"w{i}", [P, P]) for i in range(4)]
        by_k, by_v = sb("by_k", [P, 2, P]), sb("by_v", [P, 2, P])
        m_t, m_b, tq = w1, w2, w3
        kvm_hi, kvm_lo = sb("kvm_hi", [P, P], f32r), sb("kvm_lo", [P, P], f32r)
        att_hi, att_lo = sb("att_hi", [P, T], f32r), sb("att_lo", [P, T], f32r)
        ffn_hi, ffn_lo = q_hi, q_lo
        xn_hi, xn_lo = sb("xn_hi", [P, T], f32r), sb("xn_lo", [P, T], f32r)

        th = sb("th", [P, NT, E])
        sig = sb("sig", [P, NT, E])
        score = sb("score", [P, NT, E])
        group = sb("group", [P, NT, NG + 4])
        group_top = sb("group_top", [P, NT, 8])
        group_left = sb("group_left", [P, NT, NG + 4])
        group_on = sb("group_on", [P, NT, NG])
        masked = sb("masked", [P, NT, E + 2])
        top = sb("top", [P, NT, 8])
        left = sb("left", [P, NT, E + 2])
        top_sum = sb("top_sum", [P, NT])
        top_eps = sb("top_eps", [P, NT])
        top_inv = sb("top_inv", [P, NT])
        picked = sig
        comb_tok = sb("comb_tok", [P, NT, 2, E])

        cur_hi, cur_lo = sb("cur_hi", [P, T], f32r), sb("cur_lo", [P, T], f32r)
        comb = sb("comb", [P, T])
        hid_hi = [sb(f"hid_hi{i}", [P, T], f32r) for i in range(R)]
        hid_lo = [sb(f"hid_lo{i}", [P, T], f32r) for i in range(R)]
        z = sb("z", [P, T])
        z_out = sb("z_out", [P, NT, C])

        gate_ps = [ps("gate_ps0"), ps("gate_ps1")]
        up_ps = [ps("up_ps0"), ps("up_ps1")]
        y_ps = ps("y_ps")
        A = [ps("a_ps0"), ps("a_ps1"), ps("a_ps2")]

        s_proj, s_cols, s_rows, s_x, s_store = [sem(n) for n in
                                                ("proj_in", "cols_in", "rows_in", "x_in", "stored")]
        s_stage = [sem(f"stage_in{i}") for i in range(3)]
        s_cent = sem("down_centred")
        s_mean = sem("down_mean")
        s_whi, s_wlo = sem("weights_hi"), sem("weights_lo")
        s_ones, s_mat, s_const = sem("ones_set"), sem("matrices_set"), sem("constants_set")
        s_setup = sem("setup_steps")
        s_b2 = sem("b2_centred")
        s_b2c = sem("b2c_copied")
        s_phi, s_plo, s_pc = sem("proj_hi_ready"), sem("proj_lo_ready"), sem("proj_centred")
        names = ("xhi xlo kvp kvb qp qhi qlo ksq ksum kn knhi knlo_p knlo_v ktv kt1 kt2 kt3 kt4 kt5 kt6 "
                 "ktot kvm kvmhi kvmlo attp att atthi attlo p1p ffn ffnhi ffnlo p2p cen cent csq "
                 "xntok xnt xnhi xnlo rtp th sig score gmax gtop gpad gleft gon mask ktop kpad tsum "
                 "teps tinv kleft pick combt combp comb curhi curlo "
                 "z zt zcopy zsq zout").split()
        s = {n: sem("s_" + n) for n in names}
        s_newton = sem("newton_steps")
        s_gate, s_up, s_silu, s_scaled, s_hid, s_hhi, s_hlo, s_down = [
            sem(n) for n in ("gate_ready", "up_ready", "silu_done", "scaled_done", "hid_done",
                             "hid_hi_done", "hid_lo_done", "down_done")]

        block = ctx.enter_context(nc.Block())

        def wait(eng, which, value):
            if not (isinstance(value, int) and value <= 0):
                eng.wait_ge(which, value)

        def chunks_done(b, step):
            return b * NS + (step + 1)

        NEWTON = 11

        def roots_done(call):
            return NEWTON * (call + 1)

        def scaled_done(b, step):
            return b * (NS - 1) + step

        def halves(t):
            return kv[:, t, :].rearrange("p t (a c) -> p t a c", a=2)

        def kn_part(t, part):
            two = kn[:, t, :].rearrange("p t (a w) -> p t a w", a=2)
            return two[:, :, :, part * C:(part + 1) * C]

        AHEAD, AMID, BEHIND = range(3)
        PE_AT = dict(
            turn_weights=(0, BEHIND), kv_proj_0=(1, AMID), q_proj=(1, BEHIND), kv_proj_1=(2, AMID),
            k_t_v=(12, AMID), turn_y=(12, BEHIND), attend=(14, BEHIND), project_1=(16, BEHIND),
            residual_1=(19, AMID), project_2=(20, BEHIND), turn_cen=(22, BEHIND),
            turn_xn=(25, AMID), router=(26, BEHIND))
        ACT_AT = dict(
            split_x=(0, AHEAD), take_weights=(1, AHEAD), take_y=(2, BEHIND),
            square_kv_0=(2, BEHIND), square_kv_1=(3, BEHIND), split_q=(3, BEHIND),
            split_kn_0=(9, BEHIND), split_kn_1=(10, BEHIND), square_y=(13, BEHIND),
            split_kvm=(13, BEHIND), split_att=(15, BEHIND), gelu=(17, BEHIND),
            take_cen=(21, BEHIND), square_cen=(22, BEHIND), norm_1=(24, BEHIND),
            split_xn=(25, BEHIND), norm_2=(26, BEHIND), tanh=(27, BEHIND))
        POOL_AT = dict(rest_kn=(9, BEHIND), rest_att=(15, BEHIND), rest_ffn=(18, BEHIND))
        DVE_AT = dict(
            rest_x=(0, AHEAD), add_bias_0=(1, BEHIND), add_bias_1=(2, BEHIND),
            sum_squares_0=(3, BEHIND), sum_squares_1=(4, BEHIND), normalise_kv_0=(8, BEHIND),
            normalise_kv_1=(9, BEHIND), rest_kn=(10, BEHIND), rest_q=(11, BEHIND),
            scale_ktv=(12, BEHIND), add_ktv=(12, BEHIND), rest_kvm=(13, BEHIND),
            add_x=(14, BEHIND), rest_xn=(25, BEHIND), scores=(27, BEHIND),
            pick_groups=(28, BEHIND), mask_scores=(29, BEHIND), pick_experts=(30, BEHIND),
            find_experts=(31, BEHIND), weigh=(32, BEHIND))
        KV_ROOTS = {(5, AMID): (0, 0), (5, BEHIND): (1, 2), (6, AMID): (3, 3), (6, BEHIND): (4, 5),
                    (7, AMID): (6, 6), (7, BEHIND): (7, 8), (8, AMID): (9, 9),
                    (8, BEHIND): (10, 10)}
        LN_ROOTS = {(22, BEHIND): (0, 3), (23, AMID): (4, 7), (23, BEHIND): (8, 10)}

        @block.sync
        def _(sp):
            def load_x(n):
                wait(sp, s["att"], n)
                sp.dma_start(xt[:, :], x_t[n, :, :]).then_inc(s_x, 16)

            def store(b):
                sp.wait_ge(s["zout"], b + 1)
                sp.dma_start(out[b, :, :].rearrange("(t p) c -> p t c", p=P), z_out[:, :, :])\
                    .then_inc(s_store, 16)

            sp.dma_start(proj_f, proj).then_inc(s_proj, 16)
            sp.dma_start(xt[:, :], x_t[0, :, :]).then_inc(s_x, 16)
            for k in range(3 * SP3):
                m, part = k % 3, k // 3
                if k >= 3:
                    sp.wait_ge(s_wlo, k - 2)
                sp.dma_start(stage[k % 3],
                             moe_w[m, :, part * PC * P:(part + 1) * PC * P]
                             .rearrange("p (j h) -> p j h", j=PC)).then_inc(s_stage[k % 3], 16)
            load_x(1)
            with sp.Fori(1, NB - 1) as b:
                load_x(b + 1)
                store(b - 1)
            store(NB - 2)
            store(NB - 1)
            sp.wait_ge(s_store, 16 * NB)

        @block.tensor
        def _(pe):
            def three(out, w_hi, w_lo, m_hi, m_lo, start=True, stop=True):
                pe.matmul(out, w_hi, m_hi, start=start, stop=False)
                pe.matmul(out, w_hi, m_lo, start=False, stop=False)
                return pe.matmul(out, w_lo, m_hi, start=False, stop=stop)

            def weights(m, step):
                c = slice(step * P, (step + 1) * P)
                return moe_hi[m][:, c], moe_lo[m][:, c]

            def gate_up(b, step):
                if step == 0:
                    pe.wait_ge(s["curhi"], b + 1)
                    pe.wait_ge(s["curlo"], b + 1)
                    g, u = A[0], A[1]
                else:
                    g, u = gate_ps[(step - 1) % 2], up_ps[(step - 1) % 2]
                before = chunks_done(b, step - 2) if step >= 3 else chunks_done(b - 1, 30 + step)
                if step:
                    wait(pe, s_silu, before)
                three(g[:, :], *weights(0, step), cur_hi[:, :], cur_lo[:, :]).then_inc(s_gate, 1)
                if step:
                    wait(pe, s_hid, before)
                three(u[:, :], *weights(1, step), cur_hi[:, :], cur_lo[:, :]).then_inc(s_up, 1)

            def residual(b):
                wait(pe, s["z"], b)
                pe.matmul(y_ps[:, :], centre[:, :], cur_hi[:, :], start=True, stop=False)
                pe.matmul(y_ps[:, :], centre[:, :], cur_lo[:, :], start=False, stop=False)

            def down(b, step):
                pe.wait_ge(s_hhi, chunks_done(b, step))
                pe.wait_ge(s_hlo, chunks_done(b, step))
                last = three(y_ps[:, :], *weights(2, step), hid_hi[step % R][:, :],
                             hid_lo[step % R][:, :], start=False, stop=(step == NS - 1))
                last.then_inc(s_down, 1)

            def kv_proj(n, half):
                if half == 0:
                    pe.wait_ge(s["xhi"], n + 1)
                    pe.wait_ge(s["xlo"], n + 1)
                    wait(pe, s_hid, chunks_done(n - 1, 0))
                for t in range(2):
                    tok = slice((2 * half + t) * P, (2 * half + t + 1) * P)
                    o = A[half][:, t * 2 * C:(t + 1) * 2 * C]
                    w = slice(KO, KO + 2 * C)
                    pe.matmul(o, x_hi[:, tok], proj_hi[:, w], start=True, stop=False)
                    pe.matmul(o, x_lo[:, tok], proj_hi[:, w], start=False, stop=False)
                    last = pe.matmul(o, x_hi[:, tok], proj_lo[:, w], start=False, stop=True)
                last.then_inc(s["kvp"], 1)

            def q_proj(n):
                wait(pe, s["comb"], n)
                w = slice(QO, QO + C)
                three(A[2][:, :], proj_hi[:, w], proj_lo[:, w], x_hi[:, :], x_lo[:, :])\
                    .then_inc(s["qp"], 1)

            def k_t_v(n):
                pe.wait_ge(s["knhi"], 2 * n + 2)
                pe.wait_ge(s["knlo_p"], n + 1)
                pe.wait_ge(s["knlo_v"], n + 1)
                for t in range(NT):
                    for part in (K_HI, K_LO):
                        pe.matmul(A[0][:, 0:2 * C + 2], kn[:, t, part], kn[:, t, ONES.start:V.stop],
                                  start=(t == 0 and part == K_HI),
                                  stop=(t == NT - 1 and part == K_LO))
                for t in range(NT):
                    last = pe.matmul(A[1][:, 0:2 * C], ones_r[:, :], kn[:, t, V],
                                     start=(t == 0), stop=(t == NT - 1))
                last.then_inc(s["ktv"], 1)

            def attend(n):
                for name in ("kvmhi", "kvmlo", "qhi", "qlo"):
                    pe.wait_ge(s[name], n + 1)
                three(A[1][:, :], kvm_hi[:, :], kvm_lo[:, :], q_hi[:, :], q_lo[:, :])\
                    .then_inc(s["attp"], 1)

            def project_1(n):
                pe.wait_ge(s["atthi"], n + 1)
                pe.wait_ge(s["attlo"], n + 1)
                wait(pe, s["zsq"], n - 1)
                w = slice(P1O, P1O + C)
                three(A[2][:, :], proj_hi[:, w], proj_lo[:, w], att_hi[:, :], att_lo[:, :])\
                    .then_inc(s["p1p"], 1)

            def residual_1(n):
                pe.wait_ge(s["kvm"], n + 1)
                pe.matmul(A[0][:, :], centre2[:, :], x_hi[:, :], start=True, stop=False)
                pe.matmul(A[0][:, :], centre2[:, :], x_lo[:, :], start=False, stop=False)

            def project_2(n):
                pe.wait_ge(s["ffnhi"], n + 1)
                pe.wait_ge(s["ffnlo"], n + 1)
                w = slice(P2O, P2O + C)
                three(A[0][:, :], proj_hi[:, w], proj_lo[:, w], ffn_hi[:, :], ffn_lo[:, :],
                      start=False).then_inc(s["p2p"], 1)

            def turn_cen(n):
                pe.wait_ge(s["cen"], n + 1)
                for k in range(NT):
                    tok = slice(k * P, (k + 1) * P)
                    last = pe.transpose(A[1][:, tok], cen[:, tok], ident[:, :])
                last.then_inc(s["cent"], 1)

            def turn_xn(n):
                pe.wait_ge(s["xntok"], n + 1)
                for k in range(NT):
                    last = pe.transpose(A[0][:, k * P:(k + 1) * P], xn_tok[:, k, :], ident[:, :])
                last.then_inc(s["xnt"], 1)

            def router(n):
                pe.wait_ge(s["xnhi"], n + 1)
                pe.wait_ge(s["xnlo"], n + 1)
                w = slice(GO, GO + E)
                for t in range(NT):
                    tok = slice(t * P, (t + 1) * P)
                    o = A[2][:, t * E:(t + 1) * E]
                    pe.matmul(o, xn_hi[:, tok], proj_hi[:, w], start=True, stop=False)
                    pe.matmul(o, xn_lo[:, tok], proj_hi[:, w], start=False, stop=False)
                    last = pe.matmul(o, xn_hi[:, tok], proj_lo[:, w], start=False, stop=True)
                last.then_inc(s["rtp"], 1)

            def turn_weights(n):
                pe.wait_ge(s["combt"], n + 1)
                for t in range(NT):
                    last = pe.transpose(A[2][:, t * P:(t + 1) * P],
                                        comb_tok[:, t, :, :].rearrange("p r e -> p (r e)"),
                                        ident[:, :])
                last.then_inc(s["combp"], 1)

            def turn_y(b):
                pe.wait_ge(s["z"], b + 1)
                for k in range(NT):
                    tok = slice(k * P, (k + 1) * P)
                    last = pe.transpose(A[2][:, tok], z[:, tok], ident[:, :])
                last.then_inc(s["zt"], 1)

            def between(b, first, last, here):
                n = b + 1
                if PE_AT["turn_weights"] == here:
                    turn_weights(b)
                if not last:
                    if PE_AT["kv_proj_0"] == here:
                        kv_proj(n, 0)
                    if PE_AT["kv_proj_1"] == here:
                        kv_proj(n, 1)
                    if PE_AT["q_proj"] == here:
                        q_proj(n)
                    if PE_AT["k_t_v"] == here:
                        k_t_v(n)
                if PE_AT["turn_y"] == here and not first:
                    pe.wait_ge(*((s["comb"], b + 1) if last else (s["qlo"], n + 1)))
                    turn_y(b - 1)
                if not last:
                    if PE_AT["attend"] == here:
                        attend(n)
                    if PE_AT["project_1"] == here:
                        project_1(n)
                    if PE_AT["residual_1"] == here:
                        residual_1(n)
                    if PE_AT["project_2"] == here:
                        project_2(n)
                    if PE_AT["turn_cen"] == here:
                        turn_cen(n)
                    if PE_AT["turn_xn"] == here:
                        turn_xn(n)
                    if PE_AT["router"] == here:
                        router(n)

            def batch(b, first, last):
                for step in range(NS):
                    gate_up(b, step)
                    between(b, first, last, (step, AMID))
                    if step >= LAG:
                        down(b, step - LAG)
                    elif step < 2 and not first:
                        down(b - 1, step + NS - 2)
                    if step == NS - 1:
                        down(b, NS - LAG)
                    if step == 2:
                        residual(b)
                    between(b, first, last, (step, BEHIND))

            pe.wait_ge(s_mat, 1)
            pe.wait_ge(s_cols, 16)
            pe.matmul(A[2][:, 0:1], centre_f[:, :], b_2, start=True, stop=True).then_inc(s_b2, 1)
            pe.wait_ge(s_phi, 1)
            pe.wait_ge(s_plo, 1)
            kv_proj(0, 0)
            kv_proj(0, 1)
            pe.wait_ge(s_b2c, 1)
            q_proj(0)
            pe.wait_ge(s_const, 1)
            k_t_v(0)
            attend(0)
            project_1(0)
            residual_1(0)
            project_2(0)
            turn_cen(0)
            turn_xn(0)
            router(0)
            pe.wait_ge(s_wlo, 3 * SP3)
            batch(0, True, False)
            with pe.Fori(1, NB - 1) as b:
                batch(b, False, False)
            batch(NB - 1, False, True)
            for step in range(NS - 2, NS):
                down(NB - 1, step)
            turn_y(NB - 1)

        @block.scalar
        def _(act):
            def gate_act(b, step):
                act.wait_ge(s_gate, chunks_done(b, step))
                if step == R:
                    act.wait_ge(s_hid, chunks_done(b, 0))
                else:
                    wait(act, s_scaled, scaled_done(b, step - R) if step > R
                         else scaled_done(b - 1, step - R + NS))
                src = A[0] if step == 0 else gate_ps[(step - 1) % 2]
                act.activation(silu[step % R], src[:, :], ACT.Silu).then_inc(s_silu, 1)

            def hidden_hi(b, step):
                act.wait_ge(s_hid, chunks_done(b, step))
                wait(act, s_down, chunks_done(b, step - R))
                act.copy(hid_hi[step % R][:, :], hid[step % R]).then_inc(s_hhi, 1)

            def next_lo(n):
                wait(act, s_up, n * NS)
                act.wait_ge(s["xnlo"], n + 1)
                act.copy(cur_lo[:, :], xn_lo[:, :]).then_inc(s["curlo"], 1)

            def take_weights(n):
                act.wait_ge(s["combp"], n + 1)
                wait(act, s_scaled, scaled_done(n, 0))
                act.copy(comb[:, :], A[2][:, :]).then_inc(s["comb"], 1)

            def take_y(b):
                act.wait_ge(s_down, chunks_done(b, NS - 1))
                act.copy(z[:, :], y_ps[:, :]).then_inc(s["z"], 1)

            def square_y(b):
                act.wait_ge(s["zt"], b + 1)
                wait(act, s_store, 16 * b)
                act.copy(z_out[:, :, :].rearrange("p t c -> p (t c)"), A[2][:, :])\
                    .then_inc(s["zcopy"], 1)
                for k in range(NT):
                    tok = slice(k * P, (k + 1) * P)
                    last = act.activation(z[:, tok], A[2][:, tok], ACT.Square,
                                          accum_out=ssq[:, NK + k:NK + k + 1])
                last.then_inc(s["zsq"], 1)

            def norm_2(b, call):
                act.wait_ge(s_newton, roots_done(call))
                act.wait_ge(s["zcopy"], b + 1)
                for k in range(NT):
                    last = act.activation(z_out[:, k, :], z_out[:, k, :], ACT.Copy,
                                          scale=rs[:, NK + k:NK + k + 1])
                last.then_inc(s["zout"], 1)

            def split_x(n):
                act.wait_ge(s_x, 16 * n + 16)
                wait(act, s["p2p"], n)
                act.copy(x_hi[:, :], xt[:, :]).then_inc(s["xhi"], 1)

            def split_q(n):
                act.wait_ge(s["qp"], n + 1)
                act.activation(q_hi[:, :], A[2][:, :], ACT.Identity, bias=b_q).then_inc(s["qhi"], 1)

            def square_kv(n, half):
                act.wait_ge(s["kvb"], 2 * n + half + 1)
                t = slice(2 * half, 2 * half + 2)
                act.activation(kv_sq[:, t, :], kv[:, t, :], ACT.Square).then_inc(s["ksq"], 1)

            def split_kn(n, half):
                act.wait_ge(s["kn"], 2 * n + half + 1)
                t = slice(2 * half, 2 * half + 2)
                act.copy(kn_part(t, 0), halves(t)).then_inc(s["knhi"], 1)

            def split_kvm(n):
                act.wait_ge(s["kvm"], n + 1)
                act.copy(kvm_hi[:, :], kvm[:, :]).then_inc(s["kvmhi"], 1)

            def split_att(n):
                act.wait_ge(s["att"], n + 1)
                act.copy(att_hi[:, :], att).then_inc(s["atthi"], 1)

            def gelu(n):
                act.wait_ge(s["p1p"], n + 1)
                act.activation(ffn_hi[:, :], A[2][:, :], ACT.Gelu, bias=b_1).then_inc(s["ffnhi"], 1)
                act.activation(ffn, A[2][:, :], ACT.Gelu, bias=b_1).then_inc(s["ffn"], 1)

            def take_cen(n):
                act.wait_ge(s["p2p"], n + 1)
                act.activation(cen, A[0][:, :], ACT.Identity, bias=b_2c[:, :])\
                    .then_inc(s["cen"], 1)

            def square_cen(n):
                act.wait_ge(s["cent"], n + 1)
                for k in range(NT):
                    c = NK + NT + k
                    last = act.activation(xn_tok[:, k, :], A[1][:, k * P:(k + 1) * P], ACT.Square,
                                          accum_out=ssq[:, c:c + 1])
                last.then_inc(s["csq"], 1)

            def norm_1(n):
                act.wait_ge(s_newton, roots_done(2 * n + 1))
                for k in range(NT):
                    c = NK + NT + k
                    last = act.activation(xn_tok[:, k, :], A[1][:, k * P:(k + 1) * P], ACT.Copy,
                                          scale=rs[:, c:c + 1])
                last.then_inc(s["xntok"], 1)

            def split_xn(n):
                act.wait_ge(s["xnt"], n + 1)
                act.copy(xn_hi[:, :], A[0][:, :]).then_inc(s["xnhi"], 1)

            def tanh(n):
                act.wait_ge(s["rtp"], n + 1)
                act.activation(th[:, :, :], A[2][:, 0:NT * E].rearrange("p (t e) -> p t e", t=NT),
                               ACT.Tanh, scale=0.5).then_inc(s["th"], 1)

            def between(b, first, last, here):
                n = b + 1
                if not last and ACT_AT["split_x"] == here:
                    split_x(n)
                if ACT_AT["take_weights"] == here:
                    take_weights(b)
                if not first:
                    if ACT_AT["take_y"] == here:
                        take_y(b - 1)
                    if ACT_AT["square_y"] == here:
                        square_y(b - 1)
                    if ACT_AT["norm_2"] == here:
                        norm_2(b - 1, 2 * n if last else 2 * n + 1)
                if not last:
                    if ACT_AT["square_kv_0"] == here:
                        square_kv(n, 0)
                    if ACT_AT["square_kv_1"] == here:
                        square_kv(n, 1)
                    if ACT_AT["split_q"] == here:
                        split_q(n)
                    if ACT_AT["split_kn_0"] == here:
                        split_kn(n, 0)
                    if ACT_AT["split_kn_1"] == here:
                        split_kn(n, 1)
                    if ACT_AT["split_kvm"] == here:
                        split_kvm(n)
                    if ACT_AT["split_att"] == here:
                        split_att(n)
                    if ACT_AT["gelu"] == here:
                        gelu(n)
                    if ACT_AT["take_cen"] == here:
                        take_cen(n)
                    if ACT_AT["square_cen"] == here:
                        square_cen(n)
                    if ACT_AT["norm_1"] == here:
                        norm_1(n)
                    if ACT_AT["split_xn"] == here:
                        split_xn(n)
                    if ACT_AT["tanh"] == here:
                        tanh(n)

            def batch(b, first, last):
                for step in range(NS):
                    between(b, first, last, (step, AHEAD))
                    gate_act(b, step)
                    if step == NS - 1 and not last:
                        next_lo(b + 1)
                    between(b, first, last, (step, AMID))
                    if step >= 1:
                        hidden_hi(b, step - 1)
                    elif not first:
                        hidden_hi(b - 1, NS - 1)
                    between(b, first, last, (step, BEHIND))

            def split_piece(k):
                m, part = k % 3, k // 3
                if m == 2:
                    act.wait_ge(s_cent, part + 1)
                else:
                    act.wait_ge(s_stage[k % 3], 16 * (part + 1))
                act.copy(moe_hi[m][:, part * PC * P:(part + 1) * PC * P],
                         stage[k % 3].rearrange("p j h -> p (j h)")).then_inc(s_whi, 1)

            act.dma_start(col[:, :], cols).then_inc(s_cols, 16)
            act.dma_start(row[:, :], rows.partition_broadcast(P)).then_inc(s_rows, 16)
            split_x(0)
            act.wait_ge(s_pc, 2)
            act.copy(proj_hi[:, :], proj_f).then_inc(s_phi, 1)
            split_piece(0)
            split_q(0)
            square_kv(0, 0)
            square_kv(0, 1)
            split_piece(1)
            split_kn(0, 0)
            split_kn(0, 1)
            split_piece(2)
            split_piece(3)
            split_kvm(0)
            split_piece(4)
            split_att(0)
            split_piece(5)
            gelu(0)
            act.wait_ge(s_b2c, 1)
            take_cen(0)
            split_piece(6)
            square_cen(0)
            split_piece(7)
            norm_1(0)
            split_xn(0)
            split_piece(8)
            tanh(0)
            next_lo(0)
            batch(0, True, False)
            with act.Fori(1, NB - 1) as b:
                batch(b, False, False)
            batch(NB - 1, False, True)
            hidden_hi(NB - 1, NS - 1)
            take_y(NB - 1)
            square_y(NB - 1)
            norm_2(NB - 1, 2 * NB + 1)

        @block.gpsimd
        def _(pool):
            def scale(b, step):
                pool.wait_ge(s_silu, chunks_done(b, step))
                if step == 1:
                    pool.wait_ge(s["comb"], b + 1)
                wait(pool, s_hid, chunks_done(b, step - R))
                pool.tensor_tensor(scaled[step % R], silu[step % R], comb[:, :],
                                   ALU.mult).then_inc(s_scaled, 1)

            def rest(out, whole, hi, done):
                pool.tensor_tensor(out, whole, hi, ALU.subtract).then_inc(done, 1)

            def rest_kn(n):
                pool.wait_ge(s["knhi"], 2 * n + 1)
                t = slice(0, 2)
                rest(kn_part(t, 1), halves(t), kn_part(t, 0), s["knlo_p"])

            def rest_att(n):
                pool.wait_ge(s["atthi"], n + 1)
                rest(att_lo[:, :], att, att_hi[:, :], s["attlo"])

            def rest_ffn(n):
                pool.wait_ge(s["ffnhi"], n + 1)
                pool.wait_ge(s["ffn"], n + 1)
                rest(ffn_lo[:, :], ffn, ffn_hi[:, :], s["ffnlo"])

            def batch(b, first, last):
                n = b + 1
                for step in range(NS):
                    if step >= 1:
                        scale(b, step)
                    here = (step, BEHIND)
                    if not last:
                        if POOL_AT["rest_kn"] == here:
                            rest_kn(n)
                        if POOL_AT["rest_att"] == here:
                            rest_att(n)
                        if POOL_AT["rest_ffn"] == here:
                            rest_ffn(n)

            def rest_piece(k):
                m, part = k % 3, k // 3
                pool.wait_ge(s_whi, k + 1)
                wait(pool, s_wlo, k)
                rest(moe_lo[m][:, part * PC * P:(part + 1) * PC * P],
                     stage[k % 3].rearrange("p j h -> p (j h)"),
                     moe_hi[m][:, part * PC * P:(part + 1) * PC * P], s_wlo)

            pool.memset(ones_f[:, :], 1.0).then_inc(s_ones, 1)
            pool.memset(centre_f[:, :], -1.0 / P).then_inc(s_ones, 1)
            pool.memset(ident[:, :], 0.0).then_inc(s_ones, 1)
            pool.memset(blocks[:, :, :], 1.0).then_inc(s_ones, 1)
            pool.memset(kn[:, :, ONES].bitcast(fp32), 1.0).then_inc(s_ones, 1)
            pool.memset(group[:, :, NG:NG + 4], PAD).then_inc(s_ones, 1)
            pool.memset(masked[:, :, E:E + 2], PAD).then_inc(s_ones, 1)
            pool.wait_ge(s_ones, 7)
            pool.affine_select(out=centre_f[:, :], in_=centre_f[:, :], compare_op=ALU.not_equal,
                               fill=1.0 - 1.0 / P, base=0, pattern=[[-1, P]],
                               channel_multiplier=1).then_inc(s_mat, 1)
            pool.affine_select(out=ident[:, :], in_=ident[:, :], compare_op=ALU.not_equal,
                               fill=1.0, base=0, pattern=[[-1, P]],
                               channel_multiplier=1).then_inc(s_mat, 1)
            pool.affine_select(out=blocks[:, :, :], in_=blocks[:, :, :], compare_op=ALU.is_ge,
                               fill=0.0, base=0, pattern=[[-HD, NH], [0, HD]],
                               channel_multiplier=1).then_inc(s_mat, 1)
            pool.wait_ge(s_mat, 3)
            pool.affine_select(out=blocks[:, :, :], in_=blocks[:, :, :], compare_op=ALU.is_ge,
                               fill=0.0, base=HD - 1, pattern=[[HD, NH], [0, HD]],
                               channel_multiplier=-1).then_inc(s_mat, 1)
            rest_piece(0)
            rest_piece(1)
            rest_kn(0)
            rest_piece(2)
            rest_piece(3)
            rest_att(0)
            rest_piece(4)
            rest_piece(5)
            rest_ffn(0)
            rest_piece(6)
            rest_piece(7)
            rest_piece(8)
            batch(0, True, False)
            with pool.Fori(1, NB - 1) as b:
                batch(b, False, False)
            batch(NB - 1, False, True)

        @block.vector
        def _(dve):
            def product(b, step):
                if step == 0:
                    dve.wait_ge(s_silu, chunks_done(b, 0))
                    gate, up = silu[0], A[1]
                else:
                    dve.wait_ge(s_scaled, scaled_done(b, step))
                    gate, up = scaled[step % R], up_ps[(step - 1) % 2]
                dve.wait_ge(s_up, chunks_done(b, step))
                wait(dve, s_hlo, chunks_done(b, step - R))
                dve.tensor_tensor(hid[step % R], gate[:, :], up[:, :], ALU.mult)\
                    .then_inc(s_hid, 1)

            def hidden_lo(b, step):
                dve.wait_ge(s_hhi, chunks_done(b, step))
                dve.tensor_tensor(hid_lo[step % R][:, :], hid[step % R],
                                  hid_hi[step % R][:, :], ALU.subtract).then_inc(s_hlo, 1)

            def next_hi(n):
                wait(dve, s_up, n * NS)
                dve.wait_ge(s["xnhi"], n + 1)
                dve.tensor_copy(cur_hi[:, :], xn_hi[:, :]).then_inc(s["curhi"], 1)

            def rest_x(n):
                dve.wait_ge(s["xhi"], n + 1)
                dve.tensor_tensor(x_lo[:, :], xt[:, :], x_hi[:, :], ALU.subtract)\
                    .then_inc(s["xlo"], 1)

            def add_bias(n, half):
                dve.wait_ge(s["kvp"], 2 * n + half + 1)
                t = slice(2 * half, 2 * half + 2)
                dve.tensor_tensor(kv[:, t, :], A[half][:, :].rearrange("p (t c) -> p t c", t=2),
                                  b_kv.unsqueeze(1).to_broadcast([P, 2, 2 * C]), ALU.add)\
                    .then_inc(s["kvb"], 1)

            def rest_q(n):
                dve.wait_ge(s["qhi"], n + 1)
                dve.scalar_tensor_tensor(q_lo[:, :], A[2][:, :], b_q, q_hi[:, :], ALU.add,
                                         ALU.subtract).then_inc(s["qlo"], 1)

            def sum_squares(n, half):
                dve.wait_ge(s["ksq"], 2 * n + half + 1)
                t = slice(2 * half, 2 * half + 2)
                dve.tensor_reduce(ssq[:, 4 * half * NH:4 * (half + 1) * NH],
                                  kv_sq[:, t, :].rearrange("p t (g d) -> p (t g) d", d=HD),
                                  AX.X, ALU.add).then_inc(s["ksum"], 1)

            def rsqrt(call, c, means, begin, end):
                v, y, r = var[:, c], rs[:, c], tmp[:, c]
                for step in range(begin, end + 1):
                    if step > 0:
                        dve.wait_ge(s_newton, call * NEWTON + step)
                    if step == 0:
                        for cols_of, size in means:
                            last = dve.tensor_scalar(var[:, cols_of], ssq[:, cols_of], 1.0 / size,
                                                     EPS, ALU.mult, ALU.add)
                    elif step == 1:
                        last = dve.tensor_scalar(y.bitcast(i32), v.bitcast(i32), -0.5,
                                                 float(0x5f3759df), ALU.mult, ALU.add)
                    elif step % 3 == 2:
                        last = dve.scalar_tensor_tensor(r, y, -0.5, y, ALU.mult, ALU.mult)
                    elif step % 3 == 0:
                        last = dve.tensor_tensor(r, r, v, ALU.mult)
                    else:
                        last = dve.scalar_tensor_tensor(y, r, 1.5, y, ALU.add, ALU.mult)
                    last.then_inc(s_newton, 1)

            def kv_rstds(n, begin, end):
                if begin == 0:
                    dve.wait_ge(s["ksum"], 2 * n + 2)
                rsqrt(2 * n, KV, [(KV, HD)], begin, end)

            def ln_rstds(n, first, last, begin, end):
                if begin == 0 and not last:
                    dve.wait_ge(s["csq"], n + 1)
                if begin == 0 and not first:
                    dve.wait_ge(s["zsq"], n - 1)
                c = LN1 if first else LN2 if last else LNS
                rsqrt(2 * n if last else 2 * n + 1, c, [(c, C)], begin, end)

            def normalise_kv(n, half):
                dve.wait_ge(s_newton, roots_done(2 * n))
                t = slice(2 * half, 2 * half + 2)
                view = kv[:, t, :].rearrange("p t (g d) -> p (t g) d", d=HD)
                r = rs[:, 4 * half * NH:4 * (half + 1) * NH].unsqueeze(2)
                dve.tensor_tensor(view, view, r.to_broadcast([P, 4 * NH, HD]), ALU.mult)\
                    .then_inc(s["kn"], 1)

            def rest_kn(n):
                dve.wait_ge(s["knhi"], 2 * n + 2)
                t = slice(2, 4)
                dve.tensor_tensor(kn_part(t, 1), halves(t), kn_part(t, 0), ALU.subtract)\
                    .then_inc(s["knlo_v"], 1)

            def scale_ktv(n):
                dve.wait_ge(s["ktv"], n + 1)
                dve.tensor_copy(k_tot[:, :], A[0][:, 0:1]).then_inc(s["ktot"], 1)
                dve.tensor_tensor(by_k[:, :, :],
                                  A[0][:, 2:2 * C + 2].rearrange("p (a c) -> p a c", a=2),
                                  m_kv[:, :].unsqueeze(1).to_broadcast([P, 2, C]), ALU.mult)\
                    .then_inc(s["kt1"], 1)
                dve.tensor_tensor(by_v[:, :, :],
                                  A[1][:, 0:2 * C].rearrange("p (a c) -> p a c", a=2),
                                  m_v[:, :].unsqueeze(1).to_broadcast([P, 2, C]), ALU.mult)\
                    .then_inc(s["kt2"], 1)
                dve.wait_ge(s["ktot"], n + 1)
                dve.scalar_tensor_tensor(w1[:, :], m_k[:, :], k_tot[:, :], m_1[:, :], ALU.mult,
                                         ALU.add).then_inc(s["kt3"], 1)

            def add_ktv(n):
                dve.wait_ge(s["kt1"], n + 1)
                dve.tensor_tensor(w2[:, :], by_k[:, 0, :], by_k[:, 1, :], ALU.add)\
                    .then_inc(s["kt4"], 1)
                dve.wait_ge(s["kt2"], n + 1)
                dve.tensor_tensor(w3[:, :], by_v[:, 0, :], by_v[:, 1, :], ALU.add)\
                    .then_inc(s["kt5"], 1)
                dve.wait_ge(s["kt4"], n + 1)
                dve.wait_ge(s["kt3"], n + 1)
                dve.tensor_tensor(w2[:, :], w2[:, :], w1[:, :], ALU.add).then_inc(s["kt6"], 1)
                dve.wait_ge(s["kt5"], n + 1)
                dve.wait_ge(s["kt6"], n + 1)
                dve.tensor_tensor(kvm[:, :], w2[:, :], w3[:, :], ALU.add).then_inc(s["kvm"], 1)

            def rest_kvm(n):
                dve.wait_ge(s["kvmhi"], n + 1)
                dve.tensor_tensor(kvm_lo[:, :], kvm[:, :], kvm_hi[:, :], ALU.subtract)\
                    .then_inc(s["kvmlo"], 1)

            def add_x(n):
                dve.wait_ge(s["attp"], n + 1)
                dve.tensor_tensor(att, xt[:, :], A[1][:, :], ALU.add).then_inc(s["att"], 1)

            def rest_xn(n):
                dve.wait_ge(s["xnhi"], n + 1)
                dve.tensor_tensor(xn_lo[:, :], A[0][:, :], xn_hi[:, :], ALU.subtract)\
                    .then_inc(s["xnlo"], 1)

            def hold(which, value):
                dve.wait_ge(which, value)
                dve.memset(held[:, :], 0.0)

            def scores(n):
                dve.wait_ge(s["th"], n + 1)
                dve.tensor_scalar(sig[:, :, :], th[:, :, :], 0.5, 0.5, ALU.mult, ALU.add)\
                    .then_inc(s["sig"], 1)
                dve.wait_ge(s["sig"], n + 1)
                dve.tensor_tensor(score[:, :, :], sig[:, :, :],
                                  b_gate.unsqueeze(1).to_broadcast([P, NT, E]), ALU.add)\
                    .then_inc(s["score"], 1)
                dve.wait_ge(s["score"], n + 1)
                dve.tensor_reduce(group[:, :, 0:NG],
                                  score[:, :, :].rearrange("p t (g e) -> p t g e", g=NG),
                                  AX.X, ALU.max).then_inc(s["gmax"], 1)

            def pick_groups(n):
                hold(s["gmax"], n + 1)
                for t in range(NT):
                    last = dve.max(group_top[:, t, :], group[:, t, 0:NG])
                last.then_inc(s["gtop"], 1)
                dve.wait_ge(s["gtop"], n + 1)
                dve.memset(group_top[:, :, TOPG:8], PAD).then_inc(s["gpad"], 1)
                hold(s["gpad"], n + 1)
                for t in range(NT):
                    last = dve.match_replace(group_left[:, t, :], group_top[:, t, :],
                                             group[:, t, :], -PAD)
                last.then_inc(s["gleft"], 1)
                dve.wait_ge(s["gleft"], n + 1)
                dve.tensor_tensor(group_on[:, :, :], group[:, :, 0:NG], group_left[:, :, 0:NG],
                                  ALU.not_equal).then_inc(s["gon"], 1)

            def mask_scores(n):
                dve.wait_ge(s["gon"], n + 1)
                for t in range(NT):
                    last = dve.tensor_tensor(
                        masked[:, t, 0:E].rearrange("p (g e) -> p g e", g=NG),
                        score[:, t, :].rearrange("p (g e) -> p g e", g=NG),
                        group_on[:, t, :].unsqueeze(2).to_broadcast([P, NG, EG]), ALU.mult)
                last.then_inc(s["mask"], 1)

            def pick_experts(n):
                hold(s["mask"], n + 1)
                for t in range(NT):
                    last = dve.max(top[:, t, :], masked[:, t, 0:E])
                last.then_inc(s["ktop"], 1)
                dve.wait_ge(s["ktop"], n + 1)
                dve.tensor_reduce(top_sum[:, :], top[:, :, 0:TOPK], AX.X, ALU.add)\
                    .then_inc(s["tsum"], 1)
                dve.memset(top[:, :, TOPK:8], PAD).then_inc(s["kpad"], 1)

            def find_experts(n):
                hold(s["kpad"], n + 1)
                for t in range(NT):
                    last = dve.match_replace(left[:, t, :], top[:, t, :], masked[:, t, :], 0.0)
                last.then_inc(s["kleft"], 1)
                dve.wait_ge(s["tsum"], n + 1)
                dve.tensor_scalar(top_eps[:, :], top_sum[:, :], 1e-8, None, ALU.add)\
                    .then_inc(s["teps"], 1)
                dve.wait_ge(s["teps"], n + 1)
                dve.reciprocal(top_inv[:, :], top_eps[:, :]).then_inc(s["tinv"], 1)

            def weigh(n):
                dve.wait_ge(s["kleft"], n + 1)
                dve.tensor_tensor(picked[:, :, :], masked[:, :, 0:E], left[:, :, 0:E],
                                  ALU.subtract).then_inc(s["pick"], 1)
                dve.wait_ge(s["pick"], n + 1)
                dve.wait_ge(s["tinv"], n + 1)
                wait(dve, s["combp"], n)
                for r in range(2):
                    last = dve.tensor_tensor(comb_tok[:, :, r, :], picked[:, :, :],
                                             top_inv[:, :].unsqueeze(2).to_broadcast([P, NT, E]),
                                             ALU.mult)
                last.then_inc(s["combt"], 1)

            def between(b, first, last, here):
                n = b + 1
                if here in LN_ROOTS:
                    ln_rstds(n, first, last, *LN_ROOTS[here])
                if last:
                    return
                if DVE_AT["rest_x"] == here:
                    rest_x(n)
                if DVE_AT["add_bias_0"] == here:
                    add_bias(n, 0)
                if DVE_AT["add_bias_1"] == here:
                    add_bias(n, 1)
                if DVE_AT["sum_squares_0"] == here:
                    sum_squares(n, 0)
                if DVE_AT["sum_squares_1"] == here:
                    sum_squares(n, 1)
                if here in KV_ROOTS:
                    kv_rstds(n, *KV_ROOTS[here])
                if DVE_AT["normalise_kv_0"] == here:
                    normalise_kv(n, 0)
                if DVE_AT["normalise_kv_1"] == here:
                    normalise_kv(n, 1)
                if DVE_AT["rest_kn"] == here:
                    rest_kn(n)
                if DVE_AT["rest_q"] == here:
                    rest_q(n)
                if DVE_AT["scale_ktv"] == here:
                    scale_ktv(n)
                if DVE_AT["add_ktv"] == here:
                    add_ktv(n)
                if DVE_AT["rest_kvm"] == here:
                    rest_kvm(n)
                if DVE_AT["add_x"] == here:
                    add_x(n)
                if DVE_AT["rest_xn"] == here:
                    rest_xn(n)
                if DVE_AT["scores"] == here:
                    scores(n)
                if DVE_AT["pick_groups"] == here:
                    pick_groups(n)
                if DVE_AT["mask_scores"] == here:
                    mask_scores(n)
                if DVE_AT["pick_experts"] == here:
                    pick_experts(n)
                if DVE_AT["find_experts"] == here:
                    find_experts(n)
                if DVE_AT["weigh"] == here:
                    weigh(n)

            def batch(b, first, last):
                for step in range(NS):
                    between(b, first, last, (step, AHEAD))
                    if step == NS - 1 and not last:
                        next_hi(b + 1)
                    if step >= 1:
                        hidden_lo(b, step - 1)
                    elif not first:
                        hidden_lo(b - 1, NS - 1)
                    between(b, first, last, (step, AMID))
                    product(b, step)
                    between(b, first, last, (step, BEHIND))

            setup = [0]

            def chained(instruction):
                setup[0] += 1
                instruction.then_inc(s_setup, 1)
                dve.wait_ge(s_setup, setup[0])

            def centre_piece(part):
                dve.wait_ge(s_stage[2], 16 * (part + 1))
                dve.tensor_reduce(stage_mean[:, :], stage[2], AX.X, ALU.add)\
                    .then_inc(s_mean, 1)
                dve.wait_ge(s_mean, part + 1)
                dve.scalar_tensor_tensor(stage[2],
                                         stage_mean[:, :].unsqueeze(2).to_broadcast([P, PC, P]),
                                         -1.0 / P, stage[2], ALU.mult, ALU.add)\
                    .then_inc(s_cent, 1)

            w_kv = proj_f[:, KO:KO + 2 * C].rearrange("p (g d) -> p g d", d=HD)
            w_p2 = proj_f[:, P2O:P2O + C]
            dve.wait_ge(s_proj, 16)
            chained(dve.tensor_reduce(mean_kv[:, :], w_kv, AX.X, ALU.add))
            dve.scalar_tensor_tensor(w_kv, mean_kv[:, :].unsqueeze(2).to_broadcast([P, 2 * NH, HD]),
                                     -1.0 / HD, w_kv, ALU.mult, ALU.add).then_inc(s_pc, 1)
            chained(dve.tensor_reduce(mean_p2[:, :], w_p2, AX.X, ALU.add))
            chained(dve.tensor_scalar(neg_p2[:, :], mean_p2[:, :], -1.0 / C, None, ALU.mult))
            dve.tensor_scalar(w_p2, w_p2, neg_p2[:, :], None, ALU.add).then_inc(s_pc, 1)
            rest_x(0)
            dve.wait_ge(s_phi, 1)
            dve.tensor_tensor(proj_lo[:, :], proj_f, proj_hi[:, :], ALU.subtract)\
                .then_inc(s_plo, 1)
            dve.wait_ge(s_rows, 16)
            bias_kv = b_kv.rearrange("p (g d) -> p g d", d=HD)
            chained(dve.tensor_reduce(mean_b[:, :], bias_kv, AX.X, ALU.add))
            chained(dve.scalar_tensor_tensor(
                bias_kv, mean_b[:, :].unsqueeze(2).to_broadcast([P, 2 * NH, HD]), -1.0 / HD,
                bias_kv, ALU.mult, ALU.add))
            dve.wait_ge(s_b2, 1)
            dve.tensor_copy(b_2c[:, :], A[2][:, 0:1]).then_inc(s_b2c, 1)
            add_bias(0, 0)
            add_bias(0, 1)
            rest_q(0)
            sum_squares(0, 0)
            sum_squares(0, 1)
            kv_rstds(0, 0, NEWTON - 1)
            normalise_kv(0, 0)
            normalise_kv(0, 1)
            dve.wait_ge(s_mat, 4)
            dve.tensor_copy(centre[:, :], centre_f[:, :])
            dve.tensor_scalar(centre2[:, :], centre_f[:, :], 2.0, None, ALU.mult)
            dve.tensor_copy(ones_r[:, :], ones_f[:, :]).then_inc(s_const, 1)
            rest_kn(0)
            centre_piece(0)
            flat = blocks[:, :, :].rearrange("p h d -> p (h d)")
            dve.wait_ge(s_cols, 16)
            chained(dve.tensor_scalar(tq[:, :], flat, temp, 1.0 / T, ALU.mult, ALU.mult))
            dve.scalar_tensor_tensor(m_kv[:, :], tq[:, :], g_k, g_v, ALU.mult, ALU.mult)
            dve.scalar_tensor_tensor(m_k[:, :], tq[:, :], g_k, b_v, ALU.mult, ALU.mult)
            dve.scalar_tensor_tensor(m_v[:, :], tq[:, :], b_k, g_v, ALU.mult, ALU.mult)
            dve.scalar_tensor_tensor(m_t[:, :], tq[:, :], b_k, b_v, ALU.mult, ALU.mult)
            chained(dve.tensor_tensor(m_b[:, :].rearrange("p (h d) -> p h d", d=HD),
                                      blocks[:, :, :],
                                      att_bias.unsqueeze(1).to_broadcast([P, NH, HD]), ALU.mult))
            chained(dve.scalar_tensor_tensor(m_1[:, :], m_t[:, :], float(T), m_b[:, :], ALU.mult,
                                             ALU.add))
            scale_ktv(0)
            add_ktv(0)
            rest_kvm(0)
            add_x(0)
            centre_piece(1)
            ln_rstds(0, True, False, 0, NEWTON - 1)
            centre_piece(2)
            rest_xn(0)
            next_hi(0)
            scores(0)
            pick_groups(0)
            mask_scores(0)
            pick_experts(0)
            find_experts(0)
            weigh(0)
            batch(0, True, False)
            with dve.Fori(1, NB - 1) as b:
                batch(b, False, False)
            batch(NB - 1, False, True)
            hidden_lo(NB - 1, NS - 1)
            dve.wait_ge(s["zsq"], NB)
            rsqrt(2 * NB + 1, LN2, [(LN2, C)], 0, NEWTON - 1)


def kernel(**inputs):
    import numpy as np
    import concourse.bacc as bacc
    from concourse import mybir as mb
    from concourse.bass_utils import run_bass_kernel_spmd

    a = {k: np.asarray(v) for k, v in inputs.items()}
    x = a["L0_attn_x"]
    nb, t, c = x.shape
    heads = a["L0_attn_temperature"].shape[0]
    hd = c // heads
    wt = a["L0_attn_qkv_w"].T

    def units(w, k):
        e, i = w.shape[:2]
        return w.reshape(e, i // k, k, *w.shape[2:]).transpose(1, 2, 0, 3)

    def per_unit(w, shared):
        routed = units(w, 2)
        return np.concatenate([shared.T, routed.reshape(-1, c).T], axis=1)

    down = units(a["L0_ffn_ed_w"].transpose(0, 2, 1), 2)
    down = down.reshape(down.shape[0], -1, c).transpose(1, 0, 2).reshape(c, -1)
    layout = {
        "x_t": x.transpose(0, 2, 1),
        "proj": np.concatenate([wt, a["L0_attn_p1_w"].T, a["L0_attn_p2_w"].T,
                                a["L0_ffn_gate_w"].T], axis=1),
        "cols": np.concatenate([v.reshape(c, -1) for v in (
            a["L0_attn_qkv_b"][:c], a["L0_attn_p1_b"], a["L0_attn_p2_b"],
            np.repeat(a["L0_attn_temperature"].reshape(-1), hd),
            np.tile(a["L0_attn_kn_g"], heads), np.tile(a["L0_attn_kn_b"], heads),
            a["L0_attn_attn_bias"])], axis=1),
        "rows": np.concatenate([a["L0_attn_qkv_b"][c:], np.tile(a["L0_attn_vn_g"], heads),
                                np.tile(a["L0_attn_vn_b"], heads), a["L0_ffn_gate_bias"]]),
        "moe_w": np.stack([per_unit(a["L0_ffn_eg_w"], a["L0_ffn_sg_w"]),
                           per_unit(a["L0_ffn_eu_w"], a["L0_ffn_su_w"]),
                           np.concatenate([a["L0_ffn_sd_w"].T, down], axis=1)]),
    }
    nc = bacc.Bacc("TRN2", target_bir_lowering=False, num_devices=1)
    arrays, args = {}, []
    for name, v in layout.items():
        v = np.ascontiguousarray(v)
        arrays[name + "_in"] = v
        args.append(nc.dram_tensor(name + "_in", v.shape, mb.dt.from_np(v.dtype),
                                   kind="ExternalInput").ap())
    args.append(nc.dram_tensor("out", (nb, t, c), mb.dt.from_np(x.dtype),
                               kind="ExternalOutput").ap())
    post_ln_block(nc, *args)
    r = run_bass_kernel_spmd(nc, [arrays], core_ids=[0])
    return r.results[0]["out"]
```

```python
from contextlib import ExitStack

import concourse.bass as bass
from concourse import mybir


def post_ln_block(
    nc: bass.Bass,
    x_t: bass.AP,
    proj: bass.AP,
    cols: bass.AP,
    rows: bass.AP,
    moe_w: bass.AP,
    out: bass.AP,
):
    fp32 = mybir.dt.float32
    f32r = mybir.dt.float32r
    i32 = mybir.dt.int32
    ALU = mybir.AluOpType
    ACT = mybir.ActivationFunctionType
    AX = mybir.AxisListType

    NB, C, T = x_t.shape
    P = 128
    HD = 8
    NH = C // HD
    NT = T // P
    E = 64
    NG, TOPG, TOPK = 8, 4, 6
    EG = E // NG
    NS = moe_w.shape[2] // P
    SP3 = 3
    PC = NS // SP3
    PIECES = [(0, 0), (1, 0), (0, 1), (1, 1), (0, 2), (2, 0), (2, 1), (2, 2), (1, 2)]
    EPS = 1e-5
    WARM_ONES = 11
    WARM = (32, 16, 10, 7, 3, 22, 6, 9)
    PAD = -3.0e38
    LAG = 3
    R = 3
    SPARE = (0, 18)

    ctx = ExitStack()
    with ctx:
        def sb(name, shape, dt=fp32):
            return ctx.enter_context(nc.sbuf_tensor(name, shape, dt))

        def ps(name):
            return ctx.enter_context(nc.psum_tensor(name, [P, T], fp32))

        def sem(name):
            return ctx.enter_context(nc.semaphore(name))

        moe_hi = [sb(f"moe_hi{m}", [P, NS * P], f32r) for m in range(3)]
        moe_lo = [sb(f"moe_lo{m}", [P, NS * P], f32r) for m in range(3)]
        work = sb("work", [P, 3 * R, T])
        silu = [work[:, i, :] for i in range(R)]
        prod = [work[:, 2 * R + i, :] for i in range(R)]
        hid = [work[:, R + i, :] for i in range(R)]
        stage = [work[:, 3 * i:3 * i + 3, :].rearrange("p a t -> p (a t)")[:, 0:PC * P]
                 .rearrange("p (j h) -> p j h", h=P) for i in range(3)]
        stage_mean = sb("stage_mean", [P, SP3, PC])
        PW = proj.shape[1]
        QO, KO, P1O, P2O, GO = 0, C, 3 * C, 4 * C, 5 * C
        PROJ_PARTS = [[slice(KO, KO + 2 * C)], [slice(QO, QO + C), slice(P1O, PW)]]
        shared = sb("shared", [P, 2 * T])
        proj_f = shared[:, 0:PW]
        kv_sq = shared[:, :].rearrange("p (t c) -> p t c", c=2 * C)
        att, ffn = shared[:, 0:T], shared[:, T:2 * T]
        proj_hi = sb("proj_hi", [P, PW], f32r)
        proj_lo = sb("proj_lo", [P, PW], f32r)
        col = sb("col", [P, cols.shape[1]])
        b_q, b_1, b_2, temp, g_k, b_k = [col[:, i:i + 1] for i in range(6)]
        att_bias = col[:, 6:6 + HD]
        row = sb("row", [P, rows.shape[0]])
        b_kv = row[:, 0:2 * C]
        g_v, b_v = row[:, 2 * C:3 * C], row[:, 3 * C:4 * C]
        b_gate = row[:, 4 * C:4 * C + E]
        mean_kv = sb("mean_kv", [P, 2 * NH])
        mean_b = sb("mean_b", [P, 2 * NH])
        mean_p2 = sb("mean_p2", [P, 1])
        neg_p2 = sb("neg_p2", [P, 1])
        b_2c = sb("b_2c", [P, 1])

        ident = sb("ident", [P, P])
        centre_f = sb("centre_f", [P, P])
        centre = sb("centre", [P, P], f32r)
        centre2 = sb("centre2", [P, P], f32r)
        ones_f = sb("ones_f", [P, P])
        ones_r = sb("ones_r", [P, P], f32r)
        blocks = sb("blocks", [P, NH, HD])
        m_kv, m_k, m_v, m_1 = [sb(f"m_{i}", [P, P]) for i in range(4)]

        xt = sb("xt", [P, T])
        x_hi, x_lo = sb("x_hi", [P, T], f32r), sb("x_lo", [P, T], f32r)
        kv_room = sb("kv_room", [P, NT * 2 * C])
        kv = kv_room[:, :].rearrange("p (t c) -> p t c", c=2 * C)
        cen = kv_room[:, 0:T]
        xn_tok = kv_room[:, T:2 * T].rearrange("p (t c) -> p t c", c=C)
        held = sb("held", [P, 1])
        NK = NT * 2 * NH
        KV, LN2, LN1 = slice(0, NK), slice(NK, NK + NT), slice(NK + NT, NK + 2 * NT)
        LNS = slice(NK, NK + 2 * NT)
        ssq, var, tmp, rs = [sb(n, [P, NK + 2 * NT]) for n in ("ssq", "var", "tmp", "rs")]
        kn = sb("kn", [P, NT, 4 * C + 4], f32r)
        K_HI, K_LO, ONES = slice(0, C), slice(C, 2 * C), slice(2 * C, 2 * C + 2)
        V = slice(2 * C + 2, 4 * C + 2)
        q_hi, q_lo = sb("q_hi", [P, T], f32r), sb("q_lo", [P, T], f32r)
        k_tot = sb("k_tot", [P, 1])
        w1, w2, w3, kvm = [sb(f"w{i}", [P, P]) for i in range(4)]
        by_k, by_v = sb("by_k", [P, 2, P]), sb("by_v", [P, 2, P])
        m_t, m_b, tq = w1, w2, w3
        kvm_hi, kvm_lo = sb("kvm_hi", [P, P], f32r), sb("kvm_lo", [P, P], f32r)
        att_hi, att_lo = sb("att_hi", [P, T], f32r), sb("att_lo", [P, T], f32r)
        ffn_hi, ffn_lo = q_hi, q_lo
        xn_hi = [sb(f"xn_hi{i}", [P, T], f32r) for i in range(2)]
        xn_lo = [sb(f"xn_lo{i}", [P, T], f32r) for i in range(2)]

        th = sb("th", [P, NT, E])
        sig = sb("sig", [P, NT, E])
        score = sb("score", [P, NT, E])
        group = sb("group", [P, NT, NG + 4])
        group_top = sb("group_top", [P, NT, 8])
        group_left = sb("group_left", [P, NT, NG + 4])
        group_on = sb("group_on", [P, NT, NG])
        masked = sb("masked", [P, NT, E + 2])
        top = sb("top", [P, NT, 8])
        left = sb("left", [P, NT, E + 2])
        top_sum = sb("top_sum", [P, NT])
        top_eps = sb("top_eps", [P, NT])
        top_inv = sb("top_inv", [P, NT])
        picked = sig
        comb_tok = sb("comb_tok", [P, NT, 2, E])

        comb = sb("comb", [P, T])
        hid_hi = [sb(f"hid_hi{i}", [P, T], f32r) for i in range(R)]
        hid_lo = [sb(f"hid_lo{i}", [P, T], f32r) for i in range(R)]
        z = sb("z", [P, T])
        z_out = sb("z_out", [P, NT, C])

        gate_ps = [ps("gate_ps0"), ps("gate_ps1")]
        up_ps = [ps("up_ps0"), ps("up_ps1")]
        y_ps = ps("y_ps")
        A = [ps("a_ps0"), ps("a_ps1"), ps("a_ps2")]

        s_proj, s_cols, s_rows, s_x, s_store = [sem(n) for n in
                                                ("proj_in", "cols_in", "rows_in", "x_in", "stored")]
        s_stage = [sem(f"stage_in{i}") for i in range(3)]
        s_cent = sem("down_centred")
        s_mean = sem("down_mean")
        s_whi, s_wlo = sem("weights_hi"), sem("weights_lo")
        s_ones, s_mat, s_const = sem("ones_set"), sem("matrices_set"), sem("constants_set")
        s_setup = sem("setup_steps")
        s_b2 = sem("b2_centred")
        s_b2c = sem("b2c_copied")
        s_phi, s_plo, s_pc = sem("proj_hi_ready"), sem("proj_lo_ready"), sem("proj_centred")
        names = ("xhi xlo kvp kvb qp qhi qlo ksq ksum kn knhi knlo_p knlo_v ktv kt1 kt2 kt3 kt4 "
                 "kt5 kt6 ktot kvm kvmhi kvmlo attp att atthi attlo p1p ffn ffnhi ffnlo p2p "
                 "cen cent csq xntok xnt xnhi xnlo rtp th sig score gmax gtop gpad gleft gon mask "
                 "ktop kpad tsum teps tinv kleft pick combt combp comb z zt zcopy zsq zout "
                 "zhalf").split()
        s = {n: sem("s_" + n) for n in names}
        s_newton = sem("newton_steps")
        s_gate, s_up, s_silu, s_prod, s_scaled, s_hhi, s_hlo, s_down = [
            sem(n) for n in ("gate_ready", "up_ready", "silu_done", "prod_done", "scaled_done",
                             "hid_hi_done", "hid_lo_done", "down_done")]

        block = ctx.enter_context(nc.Block())

        def wait(eng, which, value):
            if not (isinstance(value, int) and value <= 0):
                eng.wait_ge(which, value)

        def chunks_done(b, step):
            return b * NS + (step + 1)

        NEWTON = 11

        def roots_done(call):
            return NEWTON * (call + 1)

        usual = [step for step in range(NS) if step not in SPARE]

        def banks(side, step):
            if step in SPARE:
                return A[0], A[1]
            k = (usual.index(step) + side * len(usual)) % 2
            return gate_ps[k], up_ps[k]

        def banks_before(b, step):
            i = usual.index(step)
            return chunks_done(b if i >= 2 else b - 1, usual[i - 2])

        def scaled_done(b, step):
            return b * (NS - 1) + step

        def halves(t):
            return kv[:, t, :].rearrange("p t (a c) -> p t a c", a=2)

        def kn_part(t, part):
            two = kn[:, t, :].rearrange("p t (a w) -> p t a w", a=2)
            return two[:, :, :, part * C:(part + 1) * C]

        AHEAD, AMID, BEHIND = range(3)
        PE_AT = dict(
            turn_weights=(1, AMID), kv_proj_0=(1, BEHIND), q_proj=(3, AMID), kv_proj_1=(2, AMID),
            k_t_v=(13, AMID), turn_y=(13, BEHIND), attend=(16, AMID), project_1=(18, BEHIND),
            residual_1=(21, BEHIND), project_2=(21, BEHIND), turn_cen=(22, AMID),
            turn_xn=(26, AMID), router=(28, BEHIND))
        PE_FIRST_AT = dict(
            PE_AT, turn_weights=(2, AMID), kv_proj_0=(2, AMID), q_proj=(3, BEHIND))
        ACT_AT = dict(
            split_x=(0, AHEAD), take_weights=(1, AMID), take_y=(1, BEHIND),
            square_kv_0=(2, BEHIND), square_kv_1=(3, BEHIND), split_q=(4, AMID),
            split_kn_0=(10, BEHIND), split_kn_1=(11, BEHIND), square_y=(15, AMID),
            split_kvm=(14, BEHIND), split_att=(16, BEHIND), gelu=(18, AMID), take_cen=(22, AHEAD),
            square_cen=(22, AMID), norm_1=(25, AMID), split_xn=(26, AMID), norm_2=(28, AHEAD),
            tanh=(29, AHEAD))
        POOL_AT = dict(
            rest_kn=(10, BEHIND))
        DVE_AT = dict(
            rest_x=(1, AHEAD), add_bias_0=(1, AMID), add_bias_1=(3, AHEAD),
            sum_squares_0=(3, BEHIND), sum_squares_1=(4, BEHIND), normalise_kv_0=(8, BEHIND),
            normalise_kv_1=(10, AMID), rest_kn=(11, BEHIND), rest_q=(12, AHEAD),
            scale_ktv=(13, BEHIND), add_ktv=(13, BEHIND), rest_kvm=(14, AMID), add_x=(16, AMID),
            rest_att=(16, BEHIND), split_ffn=(18, BEHIND), rest_xn=(27, AHEAD),
            scores=(28, BEHIND), pick_groups=(29, BEHIND), mask_scores=(29, BEHIND),
            pick_experts=(31, AHEAD), find_experts=(32, AMID), weigh=(32, BEHIND))
        KV_ROOTS = {(5, AMID): (0, 0), (5, BEHIND): (1, 2), (6, AHEAD): (3, 3), (6, AMID): (4, 4),
                    (6, BEHIND): (5, 5), (7, AMID): (6, 6), (7, BEHIND): (7, 7),
                    (8, AHEAD): (8, 8), (8, AMID): (9, 9), (8, BEHIND): (10, 10)}
        LN_ROOTS = {(22, AMID): (0, 0), (22, BEHIND): (1, 3), (23, AMID): (4, 5),
                    (23, BEHIND): (6, 6), (24, AHEAD): (7, 9), (24, AMID): (10, 10)}

        @block.sync
        def _(sp):
            def load_x(n):
                wait(sp, s["att"], n)
                sp.dma_start(xt[:, :], x_t[n, :, :]).then_inc(s_x, 16)

            def store(b):
                sp.wait_ge(s["zout"], b + 1)
                sp.dma_start(out[b, :, :].rearrange("(t p) c -> p t c", p=P), z_out[:, :, :])\
                    .then_inc(s_store, 16)

            sp.dma_start(proj_f, proj).then_inc(s_proj, 16)
            sp.dma_start(xt[:, :], x_t[0, :, :]).then_inc(s_x, 16)
            for k, (m, part) in enumerate(PIECES):
                if k == len(PIECES) - 2:
                    load_x(1)
                if k >= 3:
                    sp.wait_ge(s_wlo, k - 2)
                sp.dma_start(stage[k % 3],
                             moe_w[m, :, part * PC * P:(part + 1) * PC * P]
                             .rearrange("p (j h) -> p j h", j=PC)).then_inc(s_stage[k % 3], 16)
            with sp.Fori(1, NB - 1) as b:
                load_x(b + 1)
                store(b - 1)
            store(NB - 2)
            sp.wait_ge(s["zhalf"], 1)
            store(NB - 1)
            sp.wait_ge(s_store, 16 * NB)

        @block.tensor
        def _(pe):
            def three(out, w_hi, w_lo, m_hi, m_lo, start=True, stop=True):
                pe.matmul(out, w_hi, m_hi, start=start, stop=False)
                pe.matmul(out, w_hi, m_lo, start=False, stop=False)
                return pe.matmul(out, w_lo, m_hi, start=False, stop=stop)

            def weights(m, step):
                c = slice(step * P, (step + 1) * P)
                return moe_hi[m][:, c], moe_lo[m][:, c]

            def keep_warm(count):
                for _ in range(count):
                    pe.matmul(y_ps[:, :], proj_hi[:, 0:P], proj_hi[:, 0:T],
                              start=True, stop=True)

            def gate_up(b, side, last, step):
                if step == 0:
                    pe.wait_ge(s["xnhi"], b + 1)
                    pe.wait_ge(s["xnlo"], b + 1)
                elif step in SPARE and not last:
                    pe.wait_ge(s["att"], b + 2)
                g, u = banks(side, step)
                if step not in SPARE:
                    wait(pe, s_silu, banks_before(b, step))
                three(g[:, :], *weights(0, step), xn_hi[side][:, :], xn_lo[side][:, :])\
                    .then_inc(s_gate, 1)
                if step not in SPARE:
                    wait(pe, s_prod, banks_before(b, step))
                three(u[:, :], *weights(1, step), xn_hi[side][:, :], xn_lo[side][:, :])\
                    .then_inc(s_up, 1)

            def residual(b, side):
                wait(pe, s["z"], b)
                pe.matmul(y_ps[:, :], centre[:, :], xn_hi[side][:, :], start=True, stop=False)
                pe.matmul(y_ps[:, :], centre[:, :], xn_lo[side][:, :], start=False, stop=False)

            def down(b, step):
                pe.wait_ge(s_hhi, chunks_done(b, step))
                pe.wait_ge(s_hlo, chunks_done(b, step))
                last = three(y_ps[:, :], *weights(2, step), hid_hi[step % R][:, :],
                             hid_lo[step % R][:, :], start=False, stop=(step == NS - 1))
                last.then_inc(s_down, 1)

            def kv_proj(n, half):
                if half == 0:
                    pe.wait_ge(s["xhi"], n + 1)
                    pe.wait_ge(s["xlo"], n + 1)
                    wait(pe, s_prod, chunks_done(n - 1, 0))
                for t in range(2):
                    tok = slice((2 * half + t) * P, (2 * half + t + 1) * P)
                    o = A[half][:, t * 2 * C:(t + 1) * 2 * C]
                    w = slice(KO, KO + 2 * C)
                    pe.matmul(o, x_hi[:, tok], proj_hi[:, w], start=True, stop=False)
                    pe.matmul(o, x_lo[:, tok], proj_hi[:, w], start=False, stop=False)
                    last = pe.matmul(o, x_hi[:, tok], proj_lo[:, w], start=False, stop=True)
                last.then_inc(s["kvp"], 1)

            def q_proj(n):
                wait(pe, s["comb"], n)
                w = slice(QO, QO + C)
                three(A[2][:, :], proj_hi[:, w], proj_lo[:, w], x_hi[:, :], x_lo[:, :])\
                    .then_inc(s["qp"], 1)

            def k_t_v(n):
                pe.wait_ge(s["knhi"], 2 * n + 2)
                pe.wait_ge(s["knlo_p"], n + 1)
                pe.wait_ge(s["knlo_v"], n + 1)
                for t in range(NT):
                    for part in (K_HI, K_LO):
                        pe.matmul(A[0][:, 0:2 * C + 2], kn[:, t, part], kn[:, t, ONES.start:V.stop],
                                  start=(t == 0 and part == K_HI),
                                  stop=(t == NT - 1 and part == K_LO))
                for t in range(NT):
                    last = pe.matmul(A[1][:, 0:2 * C], ones_r[:, :], kn[:, t, V],
                                     start=(t == 0), stop=(t == NT - 1))
                last.then_inc(s["ktv"], 1)

            def attend(n):
                for name in ("kvmhi", "kvmlo", "qhi", "qlo"):
                    pe.wait_ge(s[name], n + 1)
                three(A[1][:, :], kvm_hi[:, :], kvm_lo[:, :], q_hi[:, :], q_lo[:, :])\
                    .then_inc(s["attp"], 1)

            def project_1(n):
                pe.wait_ge(s["atthi"], n + 1)
                pe.wait_ge(s["attlo"], n + 1)
                wait(pe, s["zcopy"], n - 1)
                w = slice(P1O, P1O + C)
                three(A[2][:, :], proj_hi[:, w], proj_lo[:, w], att_hi[:, :], att_lo[:, :])\
                    .then_inc(s["p1p"], 1)

            def residual_1(n):
                pe.wait_ge(s["kvm"], n + 1)
                wait(pe, s_prod, chunks_done(n - 1, SPARE[1]))
                pe.matmul(A[0][:, :], centre2[:, :], x_hi[:, :], start=True, stop=False)
                pe.matmul(A[0][:, :], centre2[:, :], x_lo[:, :], start=False, stop=False)

            def project_2(n):
                pe.wait_ge(s["ffnhi"], n + 1)
                pe.wait_ge(s["ffnlo"], n + 1)
                w = slice(P2O, P2O + C)
                three(A[0][:, :], proj_hi[:, w], proj_lo[:, w], ffn_hi[:, :], ffn_lo[:, :],
                      start=False).then_inc(s["p2p"], 1)

            def turn_cen(n):
                pe.wait_ge(s["cen"], n + 1)
                for k in range(NT):
                    tok = slice(k * P, (k + 1) * P)
                    last = pe.transpose(A[1][:, tok], cen[:, tok], ident[:, :])
                last.then_inc(s["cent"], 1)

            def turn_xn(n):
                pe.wait_ge(s["xntok"], n + 1)
                for k in range(NT):
                    last = pe.transpose(A[0][:, k * P:(k + 1) * P], xn_tok[:, k, :], ident[:, :])
                last.then_inc(s["xnt"], 1)

            def router(n, side):
                pe.wait_ge(s["xnhi"], n + 1)
                pe.wait_ge(s["xnlo"], n + 1)
                w = slice(GO, GO + E)
                for t in range(NT):
                    tok = slice(t * P, (t + 1) * P)
                    o = A[2][:, t * E:(t + 1) * E]
                    pe.matmul(o, xn_hi[side][:, tok], proj_hi[:, w], start=True, stop=False)
                    pe.matmul(o, xn_lo[side][:, tok], proj_hi[:, w], start=False, stop=False)
                    last = pe.matmul(o, xn_hi[side][:, tok], proj_lo[:, w], start=False, stop=True)
                last.then_inc(s["rtp"], 1)

            def turn_weights(n):
                pe.wait_ge(s["combt"], n + 1)
                for t in range(NT):
                    last = pe.transpose(A[2][:, t * P:(t + 1) * P],
                                        comb_tok[:, t, :, :].rearrange("p r e -> p (r e)"),
                                        ident[:, :])
                last.then_inc(s["combp"], 1)

            def turn_y(b):
                pe.wait_ge(s["z"], b + 1)
                for k in range(NT):
                    tok = slice(k * P, (k + 1) * P)
                    last = pe.transpose(A[2][:, tok], z[:, tok], ident[:, :])
                last.then_inc(s["zt"], 1)

            def between(b, side, first, last, here):
                n = b + 1
                at = PE_FIRST_AT if first else PE_AT
                if at["turn_weights"] == here:
                    if first:
                        keep_warm(WARM[-1])
                    turn_weights(b)
                if not last:
                    if at["kv_proj_0"] == here:
                        kv_proj(n, 0)
                    if at["kv_proj_1"] == here:
                        kv_proj(n, 1)
                    if at["q_proj"] == here:
                        q_proj(n)
                    if at["k_t_v"] == here:
                        k_t_v(n)
                if at["turn_y"] == here and not first:
                    pe.wait_ge(*((s["comb"], b + 1) if last else (s["qlo"], n + 1)))
                    turn_y(b - 1)
                if not last:
                    if at["attend"] == here:
                        attend(n)
                    if at["project_1"] == here:
                        project_1(n)
                    if at["residual_1"] == here:
                        residual_1(n)
                    if at["project_2"] == here:
                        project_2(n)
                    if at["turn_cen"] == here:
                        turn_cen(n)
                    if at["turn_xn"] == here:
                        turn_xn(n)
                    if at["router"] == here:
                        router(n, 1 - side)

            def batch(b, side, first, last):
                for step in range(NS):
                    gate_up(b, side, last, step)
                    between(b, side, first, last, (step, AMID))
                    if first and step == LAG:
                        pe.wait_ge(s_wlo, len(PIECES))
                    if step >= LAG:
                        down(b, step - LAG)
                    elif step < 2 and not first:
                        down(b - 1, step + NS - 2)
                    if step == NS - 1:
                        down(b, NS - LAG)
                    if step == 2:
                        residual(b, side)
                    between(b, side, first, last, (step, BEHIND))

            pe.wait_ge(s_ones, 1)
            for _ in range(WARM_ONES):
                pe.matmul(y_ps[:, 0:P], ones_f[:, :], ones_f[:, :], start=True, stop=True)
            pe.wait_ge(s_mat, 1)
            pe.wait_ge(s_cols, 16)
            pe.matmul(A[2][:, 0:1], centre_f[:, :], b_2, start=True, stop=True).then_inc(s_b2, 1)
            pe.wait_ge(s_phi, 1)
            pe.wait_ge(s_plo, 1)
            kv_proj(0, 0)
            kv_proj(0, 1)
            pe.wait_ge(s_phi, 2)
            pe.wait_ge(s_plo, 2)
            pe.wait_ge(s_b2c, 1)
            q_proj(0)
            keep_warm(WARM[0])
            pe.wait_ge(s_const, 1)
            k_t_v(0)
            keep_warm(WARM[1])
            attend(0)
            keep_warm(WARM[2])
            project_1(0)
            residual_1(0)
            keep_warm(WARM[3])
            project_2(0)
            keep_warm(WARM[4])
            turn_cen(0)
            keep_warm(WARM[5])
            turn_xn(0)
            keep_warm(WARM[6])
            router(0, 0)
            pe.wait_ge(s_wlo, 5)
            batch(0, 0, True, False)
            with pe.Fori(1, NB - 1, 2) as b:
                batch(b, 1, False, False)
                batch(b + 1, 0, False, False)
            batch(NB - 1, 1, False, True)
            for step in range(NS - 2, NS):
                down(NB - 1, step)
            turn_y(NB - 1)

        @block.scalar
        def _(act):
            def gate_act(b, side, first, step):
                act.wait_ge(s_gate, chunks_done(b, step))
                if first and step == 0:
                    act.wait_ge(s_wlo, len(PIECES) - 2)
                wait(act, s_prod, chunks_done(b, step - R))
                act.activation(silu[step % R], banks(side, step)[0][:, :], ACT.Silu)\
                    .then_inc(s_silu, 1)

            def hidden_hi(b, step):
                if step == 0:
                    act.wait_ge(s_prod, chunks_done(b, 0))
                else:
                    act.wait_ge(s_scaled, scaled_done(b, step))
                wait(act, s_down, chunks_done(b, step - R))
                act.copy(hid_hi[step % R][:, :], hid[step % R]).then_inc(s_hhi, 1)

            def take_weights(n):
                act.wait_ge(s["combp"], n + 1)
                wait(act, s_scaled, scaled_done(n, 0))
                act.copy(comb[:, :], A[2][:, :]).then_inc(s["comb"], 1)

            def take_y(b):
                act.wait_ge(s_down, chunks_done(b, NS - 1))
                act.copy(z[:, :], y_ps[:, :]).then_inc(s["z"], 1)

            def square_y(b):
                act.wait_ge(s["zt"], b + 1)
                for k in range(NT):
                    tok = slice(k * P, (k + 1) * P)
                    last = act.activation(z[:, tok], A[2][:, tok], ACT.Square,
                                          accum_out=ssq[:, NK + k:NK + k + 1])
                last.then_inc(s["zsq"], 1)
                wait(act, s_store, 16 * b)
                act.copy(z_out[:, :, :].rearrange("p t c -> p (t c)"), A[2][:, :])\
                    .then_inc(s["zcopy"], 1)

            def norm_2(b, call, tiles=NT):
                act.wait_ge(s_newton, roots_done(call))
                act.wait_ge(s["zcopy"], b + 1)
                for k in range(tiles):
                    last = act.activation(z_out[:, k, :], z_out[:, k, :], ACT.Copy,
                                          scale=rs[:, NK + k:NK + k + 1])
                last.then_inc(s["zout"], 1)

            def split_x(n):
                act.wait_ge(s_x, 16 * n + 16)
                wait(act, s["p2p"], n)
                act.copy(x_hi[:, :], xt[:, :]).then_inc(s["xhi"], 1)

            def split_q(n):
                act.wait_ge(s["qp"], n + 1)
                act.activation(q_hi[:, :], A[2][:, :], ACT.Identity, bias=b_q).then_inc(s["qhi"], 1)

            def square_kv(n, half):
                act.wait_ge(s["kvb"], 2 * n + half + 1)
                t = slice(2 * half, 2 * half + 2)
                act.activation(kv_sq[:, t, :], kv[:, t, :], ACT.Square).then_inc(s["ksq"], 1)

            def split_kn(n, half):
                act.wait_ge(s["kn"], 2 * n + half + 1)
                t = slice(2 * half, 2 * half + 2)
                act.copy(kn_part(t, 0), halves(t)).then_inc(s["knhi"], 1)

            def split_kvm(n):
                act.wait_ge(s["kvm"], n + 1)
                act.copy(kvm_hi[:, :], kvm[:, :]).then_inc(s["kvmhi"], 1)

            def split_att(n):
                act.wait_ge(s["att"], n + 1)
                act.copy(att_hi[:, :], att).then_inc(s["atthi"], 1)

            def gelu(n):
                act.wait_ge(s["p1p"], n + 1)
                act.activation(ffn, A[2][:, :], ACT.Gelu, bias=b_1).then_inc(s["ffn"], 1)

            def take_cen(n):
                act.wait_ge(s["p2p"], n + 1)
                act.activation(cen, A[0][:, :], ACT.Identity, bias=b_2c[:, :])\
                    .then_inc(s["cen"], 1)

            def square_cen(n):
                act.wait_ge(s["cent"], n + 1)
                for k in range(NT):
                    c = NK + NT + k
                    last = act.activation(xn_tok[:, k, :], A[1][:, k * P:(k + 1) * P], ACT.Square,
                                          accum_out=ssq[:, c:c + 1])
                last.then_inc(s["csq"], 1)

            def norm_1(n):
                act.wait_ge(s_newton, roots_done(2 * n + 1))
                for k in range(NT):
                    c = NK + NT + k
                    last = act.activation(xn_tok[:, k, :], A[1][:, k * P:(k + 1) * P], ACT.Copy,
                                          scale=rs[:, c:c + 1])
                last.then_inc(s["xntok"], 1)

            def split_xn(n, side):
                act.wait_ge(s["xnt"], n + 1)
                act.copy(xn_hi[side][:, :], A[0][:, :]).then_inc(s["xnhi"], 1)

            def tanh(n):
                act.wait_ge(s["rtp"], n + 1)
                act.activation(th[:, :, :], A[2][:, 0:NT * E].rearrange("p (t e) -> p t e", t=NT),
                               ACT.Tanh, scale=0.5).then_inc(s["th"], 1)

            def between(b, side, first, last, here):
                n = b + 1
                if not first and not last and ACT_AT["split_x"] == here:
                    split_x(n)
                if ACT_AT["take_weights"] == here:
                    take_weights(b)
                if not first:
                    if ACT_AT["take_y"] == here:
                        take_y(b - 1)
                    if ACT_AT["square_y"] == here:
                        square_y(b - 1)
                    if ACT_AT["norm_2"] == here:
                        norm_2(b - 1, 2 * n if last else 2 * n + 1)
                if not last:
                    if ACT_AT["square_kv_0"] == here:
                        square_kv(n, 0)
                    if ACT_AT["square_kv_1"] == here:
                        square_kv(n, 1)
                    if ACT_AT["split_q"] == here:
                        split_q(n)
                    if ACT_AT["split_kn_0"] == here:
                        split_kn(n, 0)
                    if ACT_AT["split_kn_1"] == here:
                        split_kn(n, 1)
                    if ACT_AT["split_kvm"] == here:
                        split_kvm(n)
                    if ACT_AT["split_att"] == here:
                        split_att(n)
                    if ACT_AT["gelu"] == here:
                        gelu(n)
                    if ACT_AT["take_cen"] == here:
                        take_cen(n)
                    if ACT_AT["square_cen"] == here:
                        square_cen(n)
                    if ACT_AT["norm_1"] == here:
                        norm_1(n)
                    if ACT_AT["split_xn"] == here:
                        split_xn(n, 1 - side)
                    if ACT_AT["tanh"] == here:
                        tanh(n)

            def batch(b, side, first, last):
                for step in range(NS):
                    between(b, side, first, last, (step, AHEAD))
                    gate_act(b, side, first, step)
                    between(b, side, first, last, (step, AMID))
                    if step >= 1:
                        hidden_hi(b, step - 1)
                    elif not first:
                        hidden_hi(b - 1, NS - 1)
                    between(b, side, first, last, (step, BEHIND))

            def split_piece(k):
                m, part = PIECES[k]
                if m == 2:
                    act.wait_ge(s_cent, part + 1)
                else:
                    act.wait_ge(s_stage[k % 3], 16 * (k // 3 + 1))
                act.copy(moe_hi[m][:, part * PC * P:(part + 1) * PC * P],
                         stage[k % 3].rearrange("p j h -> p (j h)")).then_inc(s_whi, 1)

            act.dma_start(col[:, :], cols).then_inc(s_cols, 16)
            act.dma_start(row[:, :], rows.partition_broadcast(P)).then_inc(s_rows, 16)
            split_x(0)
            for k, parts in enumerate(PROJ_PARTS):
                act.wait_ge(s_pc, k + 1)
                for c in parts:
                    last = act.copy(proj_hi[:, c], proj_f[:, c])
                last.then_inc(s_phi, 1)
            split_piece(0)
            square_kv(0, 0)
            square_kv(0, 1)
            split_piece(1)
            split_q(0)
            split_piece(2)
            split_kn(0, 0)
            split_kn(0, 1)
            split_piece(3)
            split_kvm(0)
            split_piece(4)
            split_att(0)
            gelu(0)
            act.wait_ge(s_b2c, 1)
            take_cen(0)
            split_piece(5)
            square_cen(0)
            split_piece(6)
            norm_1(0)
            split_xn(0, 0)
            split_x(1)
            tanh(0)
            split_piece(7)
            split_piece(8)
            batch(0, 0, True, False)
            with act.Fori(1, NB - 1, 2) as b:
                batch(b, 1, False, False)
                batch(b + 1, 0, False, False)
            batch(NB - 1, 1, False, True)
            hidden_hi(NB - 1, NS - 1)
            take_y(NB - 1)
            square_y(NB - 1)
            norm_2(NB - 1, 2 * NB + 1, NT // 2)

        @block.gpsimd
        def _(pool):
            def scale(b, step):
                pool.wait_ge(s_prod, chunks_done(b, step))
                if step == 1:
                    pool.wait_ge(s["comb"], b + 1)
                wait(pool, s_hlo, chunks_done(b, step - R))
                pool.tensor_tensor(hid[step % R], prod[step % R], comb[:, :],
                                   ALU.mult).then_inc(s_scaled, 1)

            def rest(out, whole, hi, done):
                pool.tensor_tensor(out, whole, hi, ALU.subtract).then_inc(done, 1)

            def rest_kn(n):
                pool.wait_ge(s["knhi"], 2 * n + 1)
                t = slice(0, 2)
                rest(kn_part(t, 1), halves(t), kn_part(t, 0), s["knlo_p"])

            def batch(b, side, first, last):
                n = b + 1
                for step in range(NS):
                    if step >= 1 and not (last and step == NS - 1):
                        scale(b, step)
                    here = (step, BEHIND)
                    if not last:
                        if POOL_AT["rest_kn"] == here:
                            rest_kn(n)

            def rest_piece(k):
                m, part = PIECES[k]
                pool.wait_ge(s_whi, k + 1)
                wait(pool, s_wlo, k)
                rest(moe_lo[m][:, part * PC * P:(part + 1) * PC * P],
                     stage[k % 3].rearrange("p j h -> p (j h)"),
                     moe_hi[m][:, part * PC * P:(part + 1) * PC * P], s_wlo)

            pool.memset(ones_f[:, :], 1.0).then_inc(s_ones, 1)
            pool.memset(centre_f[:, :], -1.0 / P).then_inc(s_ones, 1)
            pool.memset(ident[:, :], 0.0).then_inc(s_ones, 1)
            pool.memset(blocks[:, :, :], 1.0).then_inc(s_ones, 1)
            pool.memset(kn[:, :, ONES].bitcast(fp32), 1.0).then_inc(s_ones, 1)
            pool.memset(group[:, :, NG:NG + 4], PAD).then_inc(s_ones, 1)
            pool.memset(masked[:, :, E:E + 2], PAD).then_inc(s_ones, 1)
            pool.wait_ge(s_ones, 7)
            pool.affine_select(out=centre_f[:, :], in_=centre_f[:, :], compare_op=ALU.not_equal,
                               fill=1.0 - 1.0 / P, base=0, pattern=[[-1, P]],
                               channel_multiplier=1).then_inc(s_mat, 1)
            pool.affine_select(out=ident[:, :], in_=ident[:, :], compare_op=ALU.not_equal,
                               fill=1.0, base=0, pattern=[[-1, P]],
                               channel_multiplier=1).then_inc(s_mat, 1)
            pool.affine_select(out=blocks[:, :, :], in_=blocks[:, :, :], compare_op=ALU.is_ge,
                               fill=0.0, base=0, pattern=[[-HD, NH], [0, HD]],
                               channel_multiplier=1).then_inc(s_mat, 1)
            pool.wait_ge(s_mat, 3)
            pool.affine_select(out=blocks[:, :, :], in_=blocks[:, :, :], compare_op=ALU.is_ge,
                               fill=0.0, base=HD - 1, pattern=[[HD, NH], [0, HD]],
                               channel_multiplier=-1).then_inc(s_mat, 1)
            rest_piece(0)
            rest_piece(1)
            rest_kn(0)
            rest_piece(2)
            rest_piece(3)
            rest_piece(4)
            rest_piece(5)
            rest_piece(6)
            rest_piece(7)
            rest_piece(8)
            batch(0, 0, True, False)
            with pool.Fori(1, NB - 1, 2) as b:
                batch(b, 1, False, False)
                batch(b + 1, 0, False, False)
            batch(NB - 1, 1, False, True)

        @block.vector
        def _(dve):
            def product(b, side, first, step):
                dve.wait_ge(s_silu, chunks_done(b, step))
                dve.wait_ge(s_up, chunks_done(b, step))
                if step == 0:
                    wait(dve, s_hlo, chunks_done(b, -R))
                    if first:
                        dve.wait_ge(s_wlo, len(PIECES) - 1)
                else:
                    if first and step == 1:
                        dve.wait_ge(s_wlo, len(PIECES))
                    wait(dve, s_scaled, scaled_done(b, step - R) if step > R
                         else scaled_done(b - 1, NS - R + step % R))
                dve.tensor_tensor((hid if step == 0 else prod)[step % R], silu[step % R],
                                  banks(side, step)[1][:, :], ALU.mult).then_inc(s_prod, 1)

            def scale_last(b, step):
                dve.wait_ge(s_prod, chunks_done(b, step))
                dve.wait_ge(s["comb"], b + 1)
                dve.wait_ge(s_scaled, scaled_done(b, step - 1))
                wait(dve, s_hlo, chunks_done(b, step - R))
                dve.tensor_tensor(hid[step % R], prod[step % R], comb[:, :],
                                  ALU.mult).then_inc(s_scaled, 1)

            def hidden_lo(b, step):
                dve.wait_ge(s_hhi, chunks_done(b, step))
                dve.tensor_tensor(hid_lo[step % R][:, :], hid[step % R],
                                  hid_hi[step % R][:, :], ALU.subtract).then_inc(s_hlo, 1)

            def rest_x(n):
                dve.wait_ge(s["xhi"], n + 1)
                dve.tensor_tensor(x_lo[:, :], xt[:, :], x_hi[:, :], ALU.subtract)\
                    .then_inc(s["xlo"], 1)

            def add_bias(n, half):
                dve.wait_ge(s["kvp"], 2 * n + half + 1)
                t = slice(2 * half, 2 * half + 2)
                dve.tensor_tensor(kv[:, t, :], A[half][:, :].rearrange("p (t c) -> p t c", t=2),
                                  b_kv.unsqueeze(1).to_broadcast([P, 2, 2 * C]), ALU.add)\
                    .then_inc(s["kvb"], 1)

            def rest_q(n):
                dve.wait_ge(s["qhi"], n + 1)
                dve.scalar_tensor_tensor(q_lo[:, :], A[2][:, :], b_q, q_hi[:, :], ALU.add,
                                         ALU.subtract).then_inc(s["qlo"], 1)

            def sum_squares(n, half):
                dve.wait_ge(s["ksq"], 2 * n + half + 1)
                t = slice(2 * half, 2 * half + 2)
                dve.tensor_reduce(ssq[:, 4 * half * NH:4 * (half + 1) * NH],
                                  kv_sq[:, t, :].rearrange("p t (g d) -> p (t g) d", d=HD),
                                  AX.X, ALU.add).then_inc(s["ksum"], 1)

            def rsqrt(call, c, means, begin, end):
                v, y, r = var[:, c], rs[:, c], tmp[:, c]
                for step in range(begin, end + 1):
                    if step > 0:
                        dve.wait_ge(s_newton, call * NEWTON + step)
                    if step == 0:
                        for cols_of, size in means:
                            last = dve.tensor_scalar(var[:, cols_of], ssq[:, cols_of], 1.0 / size,
                                                     EPS, ALU.mult, ALU.add)
                    elif step == 1:
                        last = dve.tensor_scalar(y.bitcast(i32), v.bitcast(i32), -0.5,
                                                 float(0x5f3759df), ALU.mult, ALU.add)
                    elif step % 3 == 2:
                        last = dve.scalar_tensor_tensor(r, y, -0.5, y, ALU.mult, ALU.mult)
                    elif step % 3 == 0:
                        last = dve.tensor_tensor(r, r, v, ALU.mult)
                    else:
                        last = dve.scalar_tensor_tensor(y, r, 1.5, y, ALU.add, ALU.mult)
                    last.then_inc(s_newton, 1)

            def kv_rstds(n, begin, end):
                if begin == 0:
                    dve.wait_ge(s["ksum"], 2 * n + 2)
                rsqrt(2 * n, KV, [(KV, HD)], begin, end)

            def ln_rstds(n, first, last, begin, end):
                if begin == 0 and not last:
                    dve.wait_ge(s["csq"], n + 1)
                if begin == 0 and not first:
                    dve.wait_ge(s["zsq"], n - 1)
                c = LN1 if first else LN2 if last else LNS
                rsqrt(2 * n if last else 2 * n + 1, c, [(c, C)], begin, end)

            def normalise_kv(n, half):
                dve.wait_ge(s_newton, roots_done(2 * n))
                t = slice(2 * half, 2 * half + 2)
                view = kv[:, t, :].rearrange("p t (g d) -> p (t g) d", d=HD)
                r = rs[:, 4 * half * NH:4 * (half + 1) * NH].unsqueeze(2)
                dve.tensor_tensor(view, view, r.to_broadcast([P, 4 * NH, HD]), ALU.mult)\
                    .then_inc(s["kn"], 1)

            def rest_kn(n):
                dve.wait_ge(s["knhi"], 2 * n + 2)
                t = slice(2, 4)
                dve.tensor_tensor(kn_part(t, 1), halves(t), kn_part(t, 0), ALU.subtract)\
                    .then_inc(s["knlo_v"], 1)

            def scale_ktv(n):
                dve.wait_ge(s["ktv"], n + 1)
                dve.tensor_copy(k_tot[:, :], A[0][:, 0:1]).then_inc(s["ktot"], 1)
                dve.tensor_tensor(by_k[:, :, :],
                                  A[0][:, 2:2 * C + 2].rearrange("p (a c) -> p a c", a=2),
                                  m_kv[:, :].unsqueeze(1).to_broadcast([P, 2, C]), ALU.mult)\
                    .then_inc(s["kt1"], 1)
                dve.tensor_tensor(by_v[:, :, :],
                                  A[1][:, 0:2 * C].rearrange("p (a c) -> p a c", a=2),
                                  m_v[:, :].unsqueeze(1).to_broadcast([P, 2, C]), ALU.mult)\
                    .then_inc(s["kt2"], 1)
                dve.wait_ge(s["ktot"], n + 1)
                dve.scalar_tensor_tensor(w1[:, :], m_k[:, :], k_tot[:, :], m_1[:, :], ALU.mult,
                                         ALU.add).then_inc(s["kt3"], 1)

            def add_ktv(n):
                dve.wait_ge(s["kt1"], n + 1)
                dve.tensor_tensor(w2[:, :], by_k[:, 0, :], by_k[:, 1, :], ALU.add)\
                    .then_inc(s["kt4"], 1)
                dve.wait_ge(s["kt2"], n + 1)
                dve.tensor_tensor(w3[:, :], by_v[:, 0, :], by_v[:, 1, :], ALU.add)\
                    .then_inc(s["kt5"], 1)
                dve.wait_ge(s["kt4"], n + 1)
                dve.wait_ge(s["kt3"], n + 1)
                dve.tensor_tensor(w2[:, :], w2[:, :], w1[:, :], ALU.add).then_inc(s["kt6"], 1)
                dve.wait_ge(s["kt5"], n + 1)
                dve.wait_ge(s["kt6"], n + 1)
                dve.tensor_tensor(kvm[:, :], w2[:, :], w3[:, :], ALU.add).then_inc(s["kvm"], 1)

            def rest_kvm(n):
                dve.wait_ge(s["kvmhi"], n + 1)
                dve.tensor_tensor(kvm_lo[:, :], kvm[:, :], kvm_hi[:, :], ALU.subtract)\
                    .then_inc(s["kvmlo"], 1)

            def add_x(n):
                dve.wait_ge(s["attp"], n + 1)
                dve.tensor_tensor(att, xt[:, :], A[1][:, :], ALU.add).then_inc(s["att"], 1)

            def rest_att(n):
                dve.wait_ge(s["atthi"], n + 1)
                dve.tensor_tensor(att_lo[:, :], att, att_hi[:, :], ALU.subtract)\
                    .then_inc(s["attlo"], 1)

            def split_ffn(n):
                dve.wait_ge(s["ffn"], n + 1)
                dve.tensor_copy(ffn_hi[:, :], ffn).then_inc(s["ffnhi"], 1)
                dve.wait_ge(s["ffnhi"], n + 1)
                dve.tensor_tensor(ffn_lo[:, :], ffn, ffn_hi[:, :], ALU.subtract)\
                    .then_inc(s["ffnlo"], 1)

            def rest_xn(n, side):
                dve.wait_ge(s["xnhi"], n + 1)
                dve.tensor_tensor(xn_lo[side][:, :], A[0][:, :], xn_hi[side][:, :], ALU.subtract)\
                    .then_inc(s["xnlo"], 1)

            def hold(which, value):
                dve.wait_ge(which, value)
                dve.memset(held[:, :], 0.0)

            def scores(n):
                dve.wait_ge(s["th"], n + 1)
                dve.tensor_scalar(sig[:, :, :], th[:, :, :], 0.5, 0.5, ALU.mult, ALU.add)\
                    .then_inc(s["sig"], 1)
                dve.wait_ge(s["sig"], n + 1)
                dve.tensor_tensor(score[:, :, :], sig[:, :, :],
                                  b_gate.unsqueeze(1).to_broadcast([P, NT, E]), ALU.add)\
                    .then_inc(s["score"], 1)
                dve.wait_ge(s["score"], n + 1)
                dve.tensor_reduce(group[:, :, 0:NG],
                                  score[:, :, :].rearrange("p t (g e) -> p t g e", g=NG),
                                  AX.X, ALU.max).then_inc(s["gmax"], 1)

            def pick_groups(n):
                hold(s["gmax"], n + 1)
                for t in range(NT):
                    last = dve.max(group_top[:, t, :], group[:, t, 0:NG])
                last.then_inc(s["gtop"], 1)
                dve.wait_ge(s["gtop"], n + 1)
                dve.memset(group_top[:, :, TOPG:8], PAD).then_inc(s["gpad"], 1)
                hold(s["gpad"], n + 1)
                for t in range(NT):
                    last = dve.match_replace(group_left[:, t, :], group_top[:, t, :],
                                             group[:, t, :], -PAD)
                last.then_inc(s["gleft"], 1)
                dve.wait_ge(s["gleft"], n + 1)
                dve.tensor_tensor(group_on[:, :, :], group[:, :, 0:NG], group_left[:, :, 0:NG],
                                  ALU.not_equal).then_inc(s["gon"], 1)

            def mask_scores(n):
                dve.wait_ge(s["gon"], n + 1)
                dve.tensor_tensor(
                    masked[:, :, 0:E].rearrange("p t (g e) -> p t g e", g=NG),
                    score[:, :, :].rearrange("p t (g e) -> p t g e", g=NG),
                    group_on[:, :, :].unsqueeze(3).to_broadcast([P, NT, NG, EG]), ALU.mult)\
                    .then_inc(s["mask"], 1)

            def pick_experts(n):
                hold(s["mask"], n + 1)
                for t in range(NT):
                    last = dve.max(top[:, t, :], masked[:, t, 0:E])
                last.then_inc(s["ktop"], 1)
                dve.wait_ge(s["ktop"], n + 1)
                dve.tensor_reduce(top_sum[:, :], top[:, :, 0:TOPK], AX.X, ALU.add)\
                    .then_inc(s["tsum"], 1)
                dve.memset(top[:, :, TOPK:8], PAD).then_inc(s["kpad"], 1)

            def find_experts(n):
                hold(s["kpad"], n + 1)
                for t in range(NT):
                    last = dve.match_replace(left[:, t, :], top[:, t, :], masked[:, t, :], 0.0)
                last.then_inc(s["kleft"], 1)
                dve.wait_ge(s["tsum"], n + 1)
                dve.tensor_scalar(top_eps[:, :], top_sum[:, :], 1e-8, None, ALU.add)\
                    .then_inc(s["teps"], 1)
                dve.wait_ge(s["teps"], n + 1)
                dve.reciprocal(top_inv[:, :], top_eps[:, :]).then_inc(s["tinv"], 1)

            def weigh(n):
                dve.wait_ge(s["kleft"], n + 1)
                dve.tensor_tensor(picked[:, :, :], masked[:, :, 0:E], left[:, :, 0:E],
                                  ALU.subtract).then_inc(s["pick"], 1)
                dve.wait_ge(s["pick"], n + 1)
                dve.wait_ge(s["tinv"], n + 1)
                wait(dve, s["combp"], n)
                for r in range(2):
                    last = dve.tensor_tensor(comb_tok[:, :, r, :], picked[:, :, :],
                                             top_inv[:, :].unsqueeze(2).to_broadcast([P, NT, E]),
                                             ALU.mult)
                last.then_inc(s["combt"], 1)

            def between(b, side, first, last, here):
                n = b + 1
                if here in LN_ROOTS:
                    ln_rstds(n, first, last, *LN_ROOTS[here])
                if last:
                    return
                if DVE_AT["rest_x"] == here and not first:
                    rest_x(n)
                if DVE_AT["add_bias_0"] == here:
                    add_bias(n, 0)
                if DVE_AT["add_bias_1"] == here:
                    add_bias(n, 1)
                if DVE_AT["sum_squares_0"] == here:
                    sum_squares(n, 0)
                if DVE_AT["sum_squares_1"] == here:
                    sum_squares(n, 1)
                if here in KV_ROOTS:
                    kv_rstds(n, *KV_ROOTS[here])
                if DVE_AT["normalise_kv_0"] == here:
                    normalise_kv(n, 0)
                if DVE_AT["normalise_kv_1"] == here:
                    normalise_kv(n, 1)
                if DVE_AT["rest_kn"] == here:
                    rest_kn(n)
                if DVE_AT["rest_q"] == here:
                    rest_q(n)
                if DVE_AT["scale_ktv"] == here:
                    scale_ktv(n)
                if DVE_AT["add_ktv"] == here:
                    add_ktv(n)
                if DVE_AT["rest_kvm"] == here:
                    rest_kvm(n)
                if DVE_AT["add_x"] == here:
                    add_x(n)
                if DVE_AT["rest_att"] == here:
                    rest_att(n)
                if DVE_AT["split_ffn"] == here:
                    split_ffn(n)
                if DVE_AT["rest_xn"] == here:
                    rest_xn(n, 1 - side)
                if DVE_AT["scores"] == here:
                    scores(n)
                if DVE_AT["pick_groups"] == here:
                    pick_groups(n)
                if DVE_AT["mask_scores"] == here:
                    mask_scores(n)
                if DVE_AT["pick_experts"] == here:
                    pick_experts(n)
                if DVE_AT["find_experts"] == here:
                    find_experts(n)
                if DVE_AT["weigh"] == here:
                    weigh(n)

            def batch(b, side, first, last):
                for step in range(NS):
                    between(b, side, first, last, (step, AHEAD))
                    product(b, side, first, step)
                    if last and step == NS - 1:
                        scale_last(b, step)
                    between(b, side, first, last, (step, AMID))
                    if step >= 1:
                        hidden_lo(b, step - 1)
                    elif not first:
                        hidden_lo(b - 1, NS - 1)
                    between(b, side, first, last, (step, BEHIND))

            setup = [0]

            def chained(instruction):
                setup[0] += 1
                instruction.then_inc(s_setup, 1)
                dve.wait_ge(s_setup, setup[0])

            def rest_proj(k):
                dve.wait_ge(s_phi, k + 1)
                for c in PROJ_PARTS[k]:
                    last = dve.tensor_tensor(proj_lo[:, c], proj_f[:, c], proj_hi[:, c],
                                             ALU.subtract)
                last.then_inc(s_plo, 1)

            def down_mean(part):
                k = PIECES.index((2, part))
                piece = stage[k % 3]
                dve.wait_ge(s_stage[k % 3], 16 * (k // 3 + 1))
                dve.tensor_reduce(stage_mean[:, part, :], piece, AX.X, ALU.add)\
                    .then_inc(s_mean, 1)

            def centre_piece(part):
                piece = stage[PIECES.index((2, part)) % 3]
                dve.wait_ge(s_mean, part + 1)
                mean = stage_mean[:, part, :].unsqueeze(2).to_broadcast([P, PC, P])
                dve.scalar_tensor_tensor(piece, mean, -1.0 / P, piece, ALU.mult, ALU.add)\
                    .then_inc(s_cent, 1)

            w_kv = proj_f[:, KO:KO + 2 * C].rearrange("p (g d) -> p g d", d=HD)
            w_p2 = proj_f[:, P2O:P2O + C]
            dve.wait_ge(s_proj, 16)
            chained(dve.tensor_reduce(mean_kv[:, :], w_kv, AX.X, ALU.add))
            dve.scalar_tensor_tensor(w_kv, mean_kv[:, :].unsqueeze(2).to_broadcast([P, 2 * NH, HD]),
                                     -1.0 / HD, w_kv, ALU.mult, ALU.add).then_inc(s_pc, 1)
            chained(dve.tensor_reduce(mean_p2[:, :], w_p2, AX.X, ALU.add))
            chained(dve.tensor_scalar(neg_p2[:, :], mean_p2[:, :], -1.0 / C, None, ALU.mult))
            dve.tensor_scalar(w_p2, w_p2, neg_p2[:, :], None, ALU.add).then_inc(s_pc, 1)
            rest_x(0)
            rest_proj(0)
            dve.wait_ge(s_rows, 16)
            bias_kv = b_kv.rearrange("p (g d) -> p g d", d=HD)
            chained(dve.tensor_reduce(mean_b[:, :], bias_kv, AX.X, ALU.add))
            chained(dve.scalar_tensor_tensor(
                bias_kv, mean_b[:, :].unsqueeze(2).to_broadcast([P, 2 * NH, HD]), -1.0 / HD,
                bias_kv, ALU.mult, ALU.add))
            rest_proj(1)
            add_bias(0, 0)
            add_bias(0, 1)
            dve.wait_ge(s_b2, 1)
            dve.tensor_copy(b_2c[:, :], A[2][:, 0:1]).then_inc(s_b2c, 1)
            sum_squares(0, 0)
            sum_squares(0, 1)
            kv_rstds(0, 0, NEWTON - 1)
            normalise_kv(0, 0)
            normalise_kv(0, 1)
            dve.wait_ge(s_mat, 4)
            dve.tensor_copy(centre[:, :], centre_f[:, :])
            dve.tensor_scalar(centre2[:, :], centre_f[:, :], 2.0, None, ALU.mult)
            dve.tensor_copy(ones_r[:, :], ones_f[:, :]).then_inc(s_const, 1)
            rest_kn(0)
            flat = blocks[:, :, :].rearrange("p h d -> p (h d)")
            dve.wait_ge(s_cols, 16)
            dve.tensor_tensor(m_b[:, :].rearrange("p (h d) -> p h d", d=HD), blocks[:, :, :],
                              att_bias.unsqueeze(1).to_broadcast([P, NH, HD]), ALU.mult)
            chained(dve.tensor_scalar(tq[:, :], flat, temp, 1.0 / T, ALU.mult, ALU.mult))
            chained(dve.scalar_tensor_tensor(m_t[:, :], tq[:, :], b_k, b_v, ALU.mult, ALU.mult))
            dve.scalar_tensor_tensor(m_kv[:, :], tq[:, :], g_k, g_v, ALU.mult, ALU.mult)
            dve.scalar_tensor_tensor(m_k[:, :], tq[:, :], g_k, b_v, ALU.mult, ALU.mult)
            dve.scalar_tensor_tensor(m_v[:, :], tq[:, :], b_k, g_v, ALU.mult, ALU.mult)
            chained(dve.scalar_tensor_tensor(m_1[:, :], m_t[:, :], float(T), m_b[:, :], ALU.mult,
                                             ALU.add))
            scale_ktv(0)
            add_ktv(0)
            rest_kvm(0)
            rest_q(0)
            add_x(0)
            rest_att(0)
            down_mean(0)
            split_ffn(0)
            centre_piece(0)
            down_mean(1)
            centre_piece(1)
            ln_rstds(0, True, False, 0, NEWTON - 1)
            down_mean(2)
            rest_xn(0, 0)
            centre_piece(2)
            rest_x(1)
            scores(0)
            pick_groups(0)
            mask_scores(0)
            pick_experts(0)
            find_experts(0)
            weigh(0)
            batch(0, 0, True, False)
            with dve.Fori(1, NB - 1, 2) as b:
                batch(b, 1, False, False)
                batch(b + 1, 0, False, False)
            batch(NB - 1, 1, False, True)
            hidden_lo(NB - 1, NS - 1)
            dve.wait_ge(s["zsq"], NB)
            rsqrt(2 * NB + 1, LN2, [(LN2, C)], 0, NEWTON - 1)
            dve.wait_ge(s_newton, roots_done(2 * NB + 1))
            dve.wait_ge(s["zcopy"], NB)
            for k in range(NT // 2, NT):
                last = dve.tensor_scalar(z_out[:, k, :], z_out[:, k, :], rs[:, NK + k:NK + k + 1],
                                         None, ALU.mult)
            last.then_inc(s["zhalf"], 1)


def kernel(**inputs):
    import numpy as np
    import concourse.bacc as bacc
    from concourse import mybir as mb
    from concourse.bass_utils import run_bass_kernel_spmd

    a = {k: np.asarray(v) for k, v in inputs.items()}
    x = a["L0_attn_x"]
    nb, t, c = x.shape
    heads = a["L0_attn_temperature"].shape[0]
    hd = c // heads
    wt = a["L0_attn_qkv_w"].T

    def units(w, k):
        e, i = w.shape[:2]
        return w.reshape(e, i // k, k, *w.shape[2:]).transpose(1, 2, 0, 3)

    def per_unit(w, shared):
        routed = units(w, 2)
        return np.concatenate([shared.T, routed.reshape(-1, c).T], axis=1)

    down = units(a["L0_ffn_ed_w"].transpose(0, 2, 1), 2)
    down = down.reshape(down.shape[0], -1, c).transpose(1, 0, 2).reshape(c, -1)
    layout = {
        "x_t": x.transpose(0, 2, 1),
        "proj": np.concatenate([wt, a["L0_attn_p1_w"].T, a["L0_attn_p2_w"].T,
                                a["L0_ffn_gate_w"].T], axis=1),
        "cols": np.concatenate([v.reshape(c, -1) for v in (
            a["L0_attn_qkv_b"][:c], a["L0_attn_p1_b"], a["L0_attn_p2_b"],
            np.repeat(a["L0_attn_temperature"].reshape(-1), hd),
            np.tile(a["L0_attn_kn_g"], heads), np.tile(a["L0_attn_kn_b"], heads),
            a["L0_attn_attn_bias"])], axis=1),
        "rows": np.concatenate([a["L0_attn_qkv_b"][c:], np.tile(a["L0_attn_vn_g"], heads),
                                np.tile(a["L0_attn_vn_b"], heads), a["L0_ffn_gate_bias"]]),
        "moe_w": np.stack([per_unit(a["L0_ffn_eg_w"], a["L0_ffn_sg_w"]),
                           per_unit(a["L0_ffn_eu_w"], a["L0_ffn_su_w"]),
                           np.concatenate([a["L0_ffn_sd_w"].T, down], axis=1)]),
    }
    nc = bacc.Bacc("TRN2", target_bir_lowering=False, num_devices=1)
    arrays, args = {}, []
    for name, v in layout.items():
        v = np.ascontiguousarray(v)
        arrays[name + "_in"] = v
        args.append(nc.dram_tensor(name + "_in", v.shape, mb.dt.from_np(v.dtype),
                                   kind="ExternalInput").ap())
    args.append(nc.dram_tensor("out", (nb, t, c), mb.dt.from_np(x.dtype),
                               kind="ExternalOutput").ap())
    post_ln_block(nc, *args)
    r = run_bass_kernel_spmd(nc, [arrays], core_ids=[0])
    return r.results[0]["out"]
```
